# Optimizing a Trainium2 kernel written in Bass

```python
import numpy as np
import jax
import jax.numpy as jnp

def _softmax(x, axis=-1):
    return jax.nn.softmax(x, axis=axis)

def _gelu(x):
    return jax.nn.gelu(x, approximate=True)

def _silu(x):
    return jax.nn.silu(x)

def _sigmoid(x):
    return jax.nn.sigmoid(x)

def _layernorm(x, axis=-1, eps=1e-05):
    m = jnp.mean(x, axis=axis, keepdims=True)
    v = jnp.var(x, axis=axis, keepdims=True)
    return (x - m) / jnp.sqrt(v + eps)

def _scatter_add(tgt, idx, src, axis=0):
    return tgt.at[idx].add(src)

def _segment_sum(src, seg, n):
    return jax.ops.segment_sum(src, seg, n)
kernel_name = 'mk_gnn_resnorm_d2_gnn_r8_09f1d0'

def setup_inputs(seed: int=0):
    np.random.seed(seed)
    _w = jnp.asarray

    def _rec_inputs():
        import jax
        import jax.numpy as jnp
        _gk = jax.random.key(seed)
        x = -0.0003713 + 1 * jax.random.normal(jax.random.fold_in(_gk, 1), (12500, 128), jnp.float32)
        src = jax.random.randint(jax.random.fold_in(_gk, 2), (200000,), 0, 12500, jnp.int32)
        dst = jnp.minimum((12500 * jax.random.uniform(jax.random.fold_in(_gk, 3), (200000,)) ** 2.0).astype(jnp.int32), 99999)
        _o = jnp.argsort(dst, stable=True)
        src = src[_o]
        dst = dst[_o]
        edge_type_8 = jax.random.randint(jax.random.fold_in(_gk, 12), (200000,), 0, 8, jnp.int32)
        return (x, src, dst, edge_type_8)
    x, src, dst, edge_type_8 = _rec_inputs()

    def _L0_gnn_setup():
        import jax, jax.numpy as jnp
        import numpy as np
        N_NODES = 12500
        N_EDGES = 75000
        H = 128
        T = 8
        L = 2

        def _gru_cell(x, h, wih, whh, bih, bhh):
            gi = x @ wih.T + bih
            gh = h @ whh.T + bhh
            i_r, i_z, i_n = jnp.split(gi, 3, axis=-1)
            h_r, h_z, h_n = jnp.split(gh, 3, axis=-1)
            r = jax.nn.sigmoid(i_r + h_r)
            z = jax.nn.sigmoid(i_z + h_z)
            n = jnp.tanh(i_n + r * h_n)
            return (1.0 - z) * n + z * h
        key = jax.random.key(seed)
        ks = jax.random.split(key, 12)
        s = 1.0 / np.sqrt(H)
        inp = {'node_features': jax.random.normal(ks[0], (N_NODES, H), dtype=jnp.float32), 'edge_index': jax.random.randint(ks[1], (2, N_EDGES), 0, N_NODES, dtype=jnp.int64), 'edge_type': jax.random.randint(ks[2], (N_EDGES,), 0, T, dtype=jnp.int64), 'node_proj_w': jax.random.uniform(ks[3], (H, H), jnp.float32, -s, s), 'node_proj_b': jax.random.uniform(ks[4], (H,), jnp.float32, -s, s), 'edge_W': jax.random.uniform(ks[5], (L, T, H, H), jnp.float32, -s, s), 'edge_b': jax.random.uniform(ks[6], (L, T, H), jnp.float32, -s, s), 'gru_wih': jax.random.uniform(ks[7], (L, 3 * H, H), jnp.float32, -s, s), 'gru_whh': jax.random.uniform(ks[8], (L, 3 * H, H), jnp.float32, -s, s), 'gru_bih': jax.random.uniform(ks[9], (L, 3 * H), jnp.float32, -s, s), 'gru_bhh': jax.random.uniform(ks[10], (L, 3 * H), jnp.float32, -s, s), 'out_w': jax.random.uniform(ks[11], (H, H), jnp.float32, -s, s), 'out_b': jnp.zeros((H,), jnp.float32)}
        return inp
    _L0_gnn_all = _L0_gnn_setup()
    _L0_gnn_in = {k: v for k, v in _L0_gnn_all.items() if k in ('node_proj_w', 'node_proj_b', 'edge_W', 'edge_b', 'gru_wih', 'gru_whh', 'gru_bih', 'gru_bhh', 'out_w', 'out_b')}
    del _L0_gnn_all

    def _L1_gnn_setup():
        import jax, jax.numpy as jnp
        import numpy as np
        N = 6250
        E = 75000
        D = 128

        def _gcn_stack(x, row, col, norm, W1, R1, W2, R2, W3, Wh, bh):
            n = x.shape[0]

            def conv(x, W, R, act):
                h = x @ W
                msg = h[row] * norm[:, None]
                agg = jax.ops.segment_sum(msg, col, num_segments=n)
                if R is not None:
                    agg = agg + x @ R
                if act:
                    agg = jax.nn.relu(agg)
                return agg
            x = conv(x, W1, R1, True)
            x = conv(x, W2, R2, True)
            x = conv(x, W3, None, False)
            return x @ Wh + bh
        key = jax.random.key(seed)
        ks = jax.random.split(key, 10)
        scale = 1.0 / np.sqrt(D)
        inp = {'x': jax.random.normal(ks[0], (N, D), dtype=jnp.float32), 'edge_index': jax.random.randint(ks[1], (2, E), 0, N, dtype=jnp.int64), 'W1': jax.random.normal(ks[2], (D, D), dtype=jnp.float32) * scale, 'R1': jax.random.normal(ks[3], (D, D), dtype=jnp.float32) * scale, 'W2': jax.random.normal(ks[4], (D, D), dtype=jnp.float32) * scale, 'R2': jax.random.normal(ks[5], (D, D), dtype=jnp.float32) * scale, 'W3': jax.random.normal(ks[6], (D, D), dtype=jnp.float32) * scale, 'Wh': jax.random.normal(ks[7], (D, D), dtype=jnp.float32) * scale, 'bh': jnp.zeros((D,), dtype=jnp.float32)}
        return inp
    _L1_gnn_all = _L1_gnn_setup()
    _L1_gnn_in = {k: v for k, v in _L1_gnn_all.items() if k in ('W1', 'R1', 'W2', 'R2', 'W3', 'Wh', 'bh')}
    del _L1_gnn_all
    return {'x': x, 'src': src, 'dst': dst, 'edge_type_8': edge_type_8, 'L0_gnn_node_proj_w': _L0_gnn_in['node_proj_w'], 'L0_gnn_node_proj_b': _L0_gnn_in['node_proj_b'], 'L0_gnn_edge_W': _L0_gnn_in['edge_W'], 'L0_gnn_edge_b': _L0_gnn_in['edge_b'], 'L0_gnn_gru_wih': _L0_gnn_in['gru_wih'], 'L0_gnn_gru_whh': _L0_gnn_in['gru_whh'], 'L0_gnn_gru_bih': _L0_gnn_in['gru_bih'], 'L0_gnn_gru_bhh': _L0_gnn_in['gru_bhh'], 'L0_gnn_out_w': _L0_gnn_in['out_w'], 'L0_gnn_out_b': _L0_gnn_in['out_b'], 'L1_gnn_W1': _L1_gnn_in['W1'], 'L1_gnn_R1': _L1_gnn_in['R1'], 'L1_gnn_W2': _L1_gnn_in['W2'], 'L1_gnn_R2': _L1_gnn_in['R2'], 'L1_gnn_W3': _L1_gnn_in['W3'], 'L1_gnn_Wh': _L1_gnn_in['Wh'], 'L1_gnn_bh': _L1_gnn_in['bh']}

def reference(x, src, dst, edge_type_8, L0_gnn_node_proj_w, L0_gnn_node_proj_b, L0_gnn_edge_W, L0_gnn_edge_b, L0_gnn_gru_wih, L0_gnn_gru_whh, L0_gnn_gru_bih, L0_gnn_gru_bhh, L0_gnn_out_w, L0_gnn_out_b, L1_gnn_W1, L1_gnn_R1, L1_gnn_W2, L1_gnn_R2, L1_gnn_W3, L1_gnn_Wh, L1_gnn_bh):
    import jax
    import jax.numpy as jnp

    def _L0_gnn_ref(node_features, edge_index, edge_type, node_proj_w, node_proj_b, edge_W, edge_b, gru_wih, gru_whh, gru_bih, gru_bhh, out_w, out_b):
        import jax, jax.numpy as jnp
        import numpy as np
        N_NODES = 12500
        N_EDGES = 75000
        H = 128
        T = 8
        L = 2

        def _gru_cell(x, h, wih, whh, bih, bhh):
            gi = x @ wih.T + bih
            gh = h @ whh.T + bhh
            i_r, i_z, i_n = jnp.split(gi, 3, axis=-1)
            h_r, h_z, h_n = jnp.split(gh, 3, axis=-1)
            r = jax.nn.sigmoid(i_r + h_r)
            z = jax.nn.sigmoid(i_z + h_z)
            n = jnp.tanh(i_n + r * h_n)
            return (1.0 - z) * n + z * h
        num_nodes = node_features.shape[0]
        src, dst = (edge_index[0], edge_index[1])
        h = jax.nn.relu(node_features @ node_proj_w.T + node_proj_b)
        for l in range(L):
            trans = jnp.einsum('nh,tdh->tnd', h, edge_W[l])
            msgs = trans[edge_type, src]
            agg = jax.ops.segment_sum(msgs, dst, num_segments=num_nodes)
            h = _gru_cell(agg, h, gru_wih[l], gru_whh[l], gru_bih[l], gru_bhh[l])
            h = jax.nn.relu(h)
        return h @ out_w.T + out_b

    def _L1_gnn_ref(x, edge_index, W1, R1, W2, R2, W3, Wh, bh):
        import jax, jax.numpy as jnp
        import numpy as np
        N = 6250
        E = 75000
        D = 128

        def _gcn_stack(x, row, col, norm, W1, R1, W2, R2, W3, Wh, bh):
            n = x.shape[0]

            def conv(x, W, R, act):
                h = x @ W
                msg = h[row] * norm[:, None]
                agg = jax.ops.segment_sum(msg, col, num_segments=n)
                if R is not None:
                    agg = agg + x @ R
                if act:
                    agg = jax.nn.relu(agg)
                return agg
            x = conv(x, W1, R1, True)
            x = conv(x, W2, R2, True)
            x = conv(x, W3, None, False)
            return x @ Wh + bh
        n = x.shape[0]
        loops = jnp.arange(n, dtype=edge_index.dtype)
        row = jnp.concatenate([edge_index[0], loops])
        col = jnp.concatenate([edge_index[1], loops])
        deg = jax.ops.segment_sum(jnp.ones_like(col, dtype=x.dtype), col, num_segments=n)
        dinv = deg ** (-0.5)
        norm = dinv[row] * dinv[col]
        return _gcn_stack(x, row, col, norm, W1, R1, W2, R2, W3, Wh, bh)
    edge_index = jnp.stack([src, dst])
    x = _layernorm(x + _L0_gnn_ref(x, edge_index, edge_type_8, L0_gnn_node_proj_w, L0_gnn_node_proj_b, L0_gnn_edge_W, L0_gnn_edge_b, L0_gnn_gru_wih, L0_gnn_gru_whh, L0_gnn_gru_bih, L0_gnn_gru_bhh, L0_gnn_out_w, L0_gnn_out_b), axis=-1)
    x = _layernorm(x + _L1_gnn_ref(x, edge_index, L1_gnn_W1, L1_gnn_R1, L1_gnn_W2, L1_gnn_R2, L1_gnn_W3, L1_gnn_Wh, L1_gnn_bh), axis=-1)
    return x

_drawn_inputs = setup_inputs


def setup_inputs(seed=0):
    import zlib

    import numpy as np

    out = dict(_drawn_inputs(seed))
    spreads = {'L0_gnn_out_b': (0.0, 0.1), 'L1_gnn_bh': (0.0, 0.1)}
    factors = {'L0_gnn_node_proj_b': 5.389, 'L0_gnn_gru_bih': 4.605, 'L0_gnn_gru_bhh': 7.429}
    for name, (base, spread) in spreads.items():
        noise = np.random.default_rng([zlib.crc32(name.encode()), seed]).standard_normal(out[name].shape)
        drawn = base * np.exp(spread * noise) if base else spread * noise
        out[name] = jnp.asarray(drawn.astype(out[name].dtype))
    for name, factor in factors.items():
        out[name] = (out[name] * factor).astype(out[name].dtype)
    return out
```

```python
from contextlib import ExitStack

import concourse.bass as bass
from concourse import mybir
from concourse.alu_op_type import AluOpType as ALU

F32 = mybir.dt.float32
I32 = mybir.dt.int32
ACT = mybir.ActivationFunctionType
AX_X = mybir.AxisListType.X

P = 128

GROUP = 4
WINDOW_LOG2 = 7
WINDOW = 1 << WINDOW_LOG2
SLOTS = 24
HALF = SLOTS // 2
TURN_GROUPS = SLOTS // GROUP

CHUNK = 512
TILES = CHUNK // P
EPS = 1e-5


def gnn_kernel(nc, x, src, dst, edge_type, proj_w, proj_b, edge_w, gru_wih, gru_whh, gru_bih,
               gru_bhh, out_w, out_b, w1, r1, w2, r2, w3, wh, bh, out):
    nodes, feat = x.shape
    edges = src.shape[0]
    layers, types = edge_w.shape[0], edge_w.shape[1]
    gates = 3
    types_log2 = types.bit_length() - 1
    assert feat == P and types == 1 << types_log2 and types * P == 2 * CHUNK

    full_chunks = nodes // CHUNK
    tail_nodes = nodes - full_chunks * CHUNK
    assert full_chunks % 2 == 0 and 0 < tail_nodes
    chunks = full_chunks + 1
    tail_tiles = -(-tail_nodes // P)

    turns = -(-edges // (P * SLOTS))
    turns += turns % 2
    edge_tiles = turns * SLOTS
    groups = edge_tiles // GROUP
    blocks = -(-edge_tiles // P)
    full_rows = edges // P
    rest_edges = edges - full_rows * P
    sums_width = nodes + WINDOW
    assert groups <= 512

    type_tables = [nc.dram_tensor(f"type_table{u}", (nodes, types * feat), F32, kind="Internal").ap() for u in range(2)]
    conv_tables = [nc.dram_tensor(f"conv_table{u}", (nodes, feat), F32, kind="Internal").ap() for u in range(2)]
    gathered = [t.rearrange("n (t d) -> (n t) d", t=types) for t in type_tables]
    gathered += [conv_tables[0], conv_tables[1], conv_tables[0]]
    state_dram = nc.dram_tensor("state_dram", (P, nodes), F32, kind="Internal").ap()
    x1_dram = nc.dram_tensor("x1_dram", (nodes, feat), F32, kind="Internal").ap()

    with ExitStack() as ctx:
        def sb(name, shape, dt=F32):
            return ctx.enter_context(nc.sbuf_tensor(name, shape, dt))

        def sem(name):
            return ctx.enter_context(nc.semaphore(name))

        sums = sb("sums", [P, 2, sums_width])
        idx = sb("idx", [P, edge_tiles], I32)
        offset = sb("offset", [P, edge_tiles])
        group_rows = sb("group_rows", [P, groups], I32)
        base_row = group_rows[0:1, :]
        window_row = group_rows[32:33, :]
        turn_ends = group_rows[64:65, 0:chunks + 1]
        plan_cell = sb("plan_cell", [1, 4], I32)
        ident = sb("ident", [P, P])
        ones = sb("ones", [P, P])
        zero = sb("zero", [P, 1])
        eps = sb("eps", [P, 1])
        window_iota0 = sb("window_iota0", [P, WINDOW])
        window_iota = sb("window_iota", [P, WINDOW])
        proj_wt = sb("proj_wt", [P, P])
        edge_wt = sb("edge_wt", [P, layers, types * P])
        gru_wt = sb("gru_wt", [P, layers, 2, gates * P])
        out_wt = sb("out_wt", [P, P])
        conv_w = sb("conv_w", [P, 6, P])
        proj_bias = sb("proj_bias", [P, 1])
        gate_bias = sb("gate_bias", [P, layers, 2, gates])
        rz_bias = sb("rz_bias", [P, layers, 2])
        bias_rows = sb("bias_rows", [1, 2, P])

        idx_ring = sb("idx_ring", [P, 2, SLOTS], I32)
        stat = sb("stat", [P, TILES, 6])
        moments = sb("moments", [P, TILES, 2])
        rstd = sb("rstd", [P, TILES])

        rows = sb("rows", [P, SLOTS, feat])
        onehot = sb("onehot", [P, 2, GROUP, WINDOW])

        nodes_region = sb("nodes_region", [P, (2 + 2 + 4) * CHUNK + 2 * types * P])
        node_in = nodes_region[:, 0:2 * CHUNK].rearrange("p (u j d) -> p u j d", u=2, d=P)
        left = nodes_region[:, 2 * CHUNK:4 * CHUNK].rearrange("p (u n) -> p u n", u=2)
        tmp = nodes_region[:, 4 * CHUNK:8 * CHUNK].rearrange("p (u n) -> p u n", u=4)
        wide = nodes_region[:, 8 * CHUNK:8 * CHUNK + 2 * types * P].rearrange("p (u n) -> p u n", u=2)
        state_in = sb("state_in", [P, 2, CHUNK])
        state_out = sb("state_out", [P, 2, CHUNK])
        n_raw = layers * (types + 2 * gates) + 2
        raw_w = nodes_region[:, 0:n_raw * P].rearrange("p (k d) -> p k d", d=P)

        stage_words = blocks * P
        sums_flat = sums[:, :, :].rearrange("p a n -> p (a n)")
        stage_int = sums_flat[:, 0:3 * stage_words].bitcast(I32).rearrange("p (k b e) -> p k b e", k=3, e=P)
        stage_f = sums_flat[:, 3 * stage_words:6 * stage_words].rearrange("p (k b e) -> p k b e", k=3, e=P)
        stage_dst_f, stage_src_f, stage_type_f = stage_f[:, 0], stage_f[:, 1], stage_f[:, 2]
        extremes = sums_flat[:, 6 * stage_words:6 * stage_words + 2 * blocks].rearrange("p (k b) -> p k b", k=2)
        at_row = 6 * stage_words + 2 * blocks

        def row_part(words):
            nonlocal at_row
            at_row += words
            assert at_row <= 2 * sums_width
            return sums_flat[0:1, at_row - words:at_row]

        ext_row = row_part(2 * stage_words).rearrange("p (k n) -> p k n", k=2)
        group_row = row_part(2 * groups).rearrange("p (k n) -> p k n", k=2)
        turn_row = row_part(turns)
        before_row = row_part(chunks * turns).rearrange("p (c i) -> p c i", c=chunks)
        chunk_end_row = row_part(chunks)
        end_row = row_part(chunks + 1)
        check_row = row_part(chunks + turns)
        plan_row = row_part(8)

        bank = ctx.enter_context(nc.psum_tensor("bank", [P, 8, 512], F32))

        staged_zero = sem("staged_zero")
        edges_in = sem("edges_in")
        weights_in = sem("weights_in")
        raw_in = sem("raw_in")
        raw_turned = sem("raw_turned")
        raw_used = sem("raw_used")
        ident_zero = sem("ident_zero")
        const_ready = sem("const_ready")
        as_float = sem("as_float")
        turned = sem("turned")
        turn_out = sem("turn_out")
        ext_made = sem("ext_made")
        ext_turned = sem("ext_turned")
        ext_out = sem("ext_out")
        group_step = sem("group_step")
        base_spread = sem("base_spread")
        phase_done = sem("phase_done")
        dinv_ready = sem("dinv_ready")

        group_done = sem("group_done")
        idx_ready = sem("idx_ready")
        onehot_ready = sem("onehot_ready")
        sums_added = sem("sums_added")
        windows_set = sem("windows_set")
        gate_passed = sem("gate_passed")
        row_landed = [sem(f"row_landed_{k}") for k in range(SLOTS)]

        phases_passed = {}

        def barrier(eng, name):
            n = phases_passed.get(name, 0) + 1
            phases_passed[name] = n
            eng.drain().then_inc(phase_done, 1)
            eng.wait_ge(phase_done, 5 * n)

        def gate(eng, *waits):
            for semaphore, count in waits:
                eng.wait_ge(semaphore, count)
                eng.sem_inc(gate_passed, 1)

        def width(c):
            return tail_nodes if isinstance(c, int) and c == full_chunks else CHUNK

        def tiles_of(c):
            n = width(c)
            return [(j, j * P, min(P, n - j * P)) for j in range(-(-n // P))]

        def cols(c, n=None):
            return bass.ds(c * CHUNK, width(c) if n is None else n)

        def sweep(eng, stages):
            most = max(lag for _, lag in stages)
            first = most + 2 + most % 2
            for s in range(first):
                for stage, lag in stages:
                    if s - lag >= 0:
                        stage(s - lag, (s - lag) % 2)
            with eng.Fori(first // 2, full_chunks // 2) as pair:
                for u in range(2):
                    for stage, lag in stages:
                        stage(pair * 2 + (u - lag), (u - lag) % 2)
            for s in range(full_chunks, chunks + most):
                for stage, lag in stages:
                    if s - lag < chunks:
                        stage(s - lag, (s - lag) % 2)

        def reuse(eng, semaphore, c, depth=1, per=1, more=0):
            if not isinstance(c, int) or c >= depth:
                eng.wait_ge(semaphore, (c - depth) * per + (per if not more else more))

        def move_rows(eng, c, table, buf, load, semaphore):
            if width(c) == CHUNK:
                d = table[bass.ds(c * CHUNK, CHUNK), :].rearrange("(j p) d -> p j d", p=P)
                eng.dma_start(buf if load else d, d if load else buf).then_inc(semaphore, 16)
                return
            for j, at, n in tiles_of(c):
                d = table[c * CHUNK + at:c * CHUNK + at + n, :]
                buf_j = buf[0:n, j, :]
                eng.dma_start(buf_j if load else d, d if load else buf_j).then_inc(semaphore, 16)

        def moves(c, q):
            if isinstance(c, int):
                return sum(1 if width(k) == CHUNK else tail_tiles for k in range(q, c + 1, 2))
            return None


        conv_ws = [w1, r1, w2, r2, w3, wh]
        raw_blocks = [(proj_w, proj_wt[:, :]), (out_w, out_wt[:, :])]
        for layer in range(layers):
            raw_blocks += [(edge_w[layer, t], edge_wt[:, layer, t * P:(t + 1) * P]) for t in range(types)]
            for k, w in enumerate((gru_wih, gru_whh)):
                raw_blocks += [(w[layer, g * P:(g + 1) * P, :], gru_wt[:, layer, k, g * P:(g + 1) * P])
                               for g in range(gates)]
        assert len(raw_blocks) == n_raw <= 32

        def raw_bank(k):
            return bank[:, k // 4, (k % 4) * P:(k % 4 + 1) * P]

        last = blocks - 1
        last_full = full_rows - last * P
        assert 0 <= last_full < P and blocks * P >= edge_tiles

        def setup_sync(sp):
            sp.wait_ge(staged_zero, 3)
            for k, a in enumerate((dst, src, edge_type)):
                body = a[0:last * P * P].rearrange("(b p e) -> p b e", p=P, e=P)
                sp.dma_start(stage_int[:, k, 0:last, :], body).then_inc(edges_in, 16)
                if last_full:
                    sp.dma_start(stage_int[0:last_full, k, last, :],
                                 a[last * P * P:full_rows * P].rearrange("(p e) -> p e", e=P)).then_inc(edges_in, 16)
                if rest_edges:
                    sp.dma_start(stage_int[last_full:last_full + 1, k, last, 0:rest_edges],
                                 a[full_rows * P:edges].rearrange("(p e) -> p e", p=1)).then_inc(edges_in, 16)
            for k, (block_in, _) in enumerate(raw_blocks):
                sp.dma_start(raw_w[:, k, :], block_in).then_inc(raw_in, 16)
            for k, w in enumerate(conv_ws):
                sp.dma_start(conv_w[:, k, :], w).then_inc(weights_in, 16)
            sp.dma_start(proj_bias[:, :], proj_b.rearrange("(p a) -> p a", a=1)).then_inc(weights_in, 16)
            for layer in range(layers):
                for k, b in enumerate((gru_bih, gru_bhh)):
                    for g in range(gates):
                        sp.dma_start(gate_bias[:, layer, k, g:g + 1],
                                     b[layer, g * P:(g + 1) * P].rearrange("(p a) -> p a", a=1)).then_inc(weights_in, 16)
            for k, b in enumerate((out_b, bh)):
                sp.dma_start(bias_rows[0:1, k, :], b.rearrange("(a n) -> a n", a=1)).then_inc(weights_in, 16)

        n_edge_loads = 3 * (1 + (last_full > 0) + (rest_edges > 0))
        n_weight_loads = len(conv_ws) + 1 + layers * 2 * gates + 2

        def setup_pool(pool):
            for k, value in enumerate((nodes, 0, 0)):
                pool.memset(stage_int[:, k, last, :], value).then_inc(staged_zero, 1)
            pool.iota(chunk_end_row, [[CHUNK, chunks]], base=CHUNK, channel_multiplier=0,
                      allow_small_or_imprecise_dtypes=True)
            pool.iota(window_iota0[:, :], [[1, WINDOW]], base=0, channel_multiplier=0,
                      allow_small_or_imprecise_dtypes=True).then_inc(const_ready, 1)
            pool.memset(zero[:, :], 0.0)
            pool.memset(eps[:, :], EPS)
            pool.memset(ones[:, :], 1.0).then_inc(const_ready, 1)
            pool.memset(ident[:, :], 0.0).then_inc(ident_zero, 1)
            pool.wait_ge(ident_zero, 1)
            pool.affine_select(out=ident[:, :], in_=ident[:, :], compare_op=ALU.not_equal, fill=1.0, base=0,
                               pattern=[[-1, P]], channel_multiplier=1).then_inc(const_ready, 1)

        turn_from = [stage_dst_f, stage_type_f]
        turn_to = [offset, idx]

        def block_tiles(b):
            return min(P, edge_tiles - b * P)

        def setup_vector(dve):
            dve.wait_ge(edges_in, 16 * n_edge_loads)
            for k in range(3):
                dve.tensor_copy(stage_f[:, k], stage_int[:, k]).then_inc(as_float, 1)
            dve.wait_ge(as_float, 3)
            dve.scalar_tensor_tensor(out=stage_type_f, in0=stage_src_f, scalar=float(types), in1=stage_type_f,
                                     op0=ALU.mult, op1=ALU.add).then_inc(as_float, 1)
            dve.tensor_reduce(extremes[:, 0, :], stage_dst_f, AX_X, ALU.min).then_inc(ext_made, 1)
            dve.tensor_reduce(extremes[:, 1, :], stage_dst_f, AX_X, ALU.max).then_inc(ext_made, 1)
            dve.wait_ge(weights_in, 16 * n_weight_loads)
            dve.tensor_tensor(rz_bias[:, :, :], gate_bias[:, :, 0, 0:2], gate_bias[:, :, 1, 0:2], ALU.add)
            for n in range(2 * blocks):
                b, k = n // 2, n % 2
                dve.wait_ge(turned, n + 1)
                dve.tensor_copy(turn_to[k][:, b * P:b * P + block_tiles(b)],
                                bank[:, 4 + n % 4, 0:block_tiles(b)]).then_inc(turn_out, 1)
            for n in range(2 * blocks):
                b, k = n // 2, n % 2
                dve.wait_ge(ext_turned, n + 1)
                dve.tensor_copy(ext_row[:, k, b * P:(b + 1) * P], bank[0:1, 4 + n % 4, 0:P]).then_inc(ext_out, 1)
            dve.wait_ge(ext_out, 2 * blocks)
            for k, op in enumerate((ALU.min, ALU.max)):
                dve.tensor_reduce(group_row[:, k, :],
                                  ext_row[:, k, 0:edge_tiles].rearrange("p (g t) -> p g t", t=GROUP),
                                  AX_X, op).then_inc(group_step, 1)
            dve.wait_ge(group_step, 2)
            dve.tensor_copy(base_row, group_row[:, 0, :]).then_inc(group_step, 1)
            dve.tensor_tensor(group_row[:, 1, :], group_row[:, 1, :], group_row[:, 0, :],
                              ALU.subtract).then_inc(group_step, 1)
            dve.tensor_reduce(turn_row, group_row[:, 0, :].rearrange("p (i g) -> p i g", g=TURN_GROUPS),
                              AX_X, ALU.min).then_inc(group_step, 1)
            dve.wait_ge(group_step, 5)
            dve.tensor_reduce(plan_row[:, 0:1], group_row[:, 1, :], AX_X, ALU.max).then_inc(group_step, 1)
            dve.wait_ge(group_step, 6)
            dve.tensor_copy(plan_cell[0:1, 2:3], plan_row[:, 0:1]).then_inc(group_step, 1)
            dve.wait_ge(group_step, 7)
            dve.tensor_single_scalar(plan_cell[0:1, 3:4], plan_cell[0:1, 2:3], WINDOW_LOG2,
                                     ALU.logical_shift_right).then_inc(group_step, 1)
            dve.wait_ge(group_step, 8)
            dve.tensor_scalar(plan_cell[0:1, 0:1], plan_cell[0:1, 3:4], 1.0, None, ALU.add).then_inc(group_step, 1)
            shape = [1, chunks, turns]
            dve.tensor_tensor(before_row, turn_row.rearrange("p (c i) -> p c i", c=1).broadcast_to(shape),
                              chunk_end_row.rearrange("p (c i) -> p c i", i=1).broadcast_to(shape),
                              ALU.is_lt).then_inc(group_step, 1)
            dve.memset(end_row[:, 0:1], 0.0)
            dve.wait_ge(group_step, 10)
            dve.tensor_reduce(end_row[:, 1:chunks + 1], before_row, AX_X, ALU.add).then_inc(group_step, 1)
            dve.wait_ge(group_step, 11)
            dve.memset(end_row[:, chunks:chunks + 1], float(turns)).then_inc(group_step, 1)
            dve.wait_ge(group_step, 12)
            dve.tensor_copy(turn_ends, end_row).then_inc(group_step, 1)
            dve.tensor_tensor(check_row[:, 0:chunks], end_row[:, 1:chunks + 1], end_row[:, 0:chunks],
                              ALU.subtract).then_inc(group_step, 1)
            dve.tensor_tensor(check_row[:, chunks:chunks + turns - 1], turn_row[:, 1:turns],
                              turn_row[:, 0:turns - 1], ALU.subtract).then_inc(group_step, 1)
            dve.tensor_scalar(check_row[:, chunks + turns - 1:chunks + turns], plan_row[:, 0:1], -1.0,
                              float(WINDOW - 1), ALU.mult, ALU.add).then_inc(group_step, 1)
            dve.wait_ge(group_step, 16)
            dve.tensor_scalar(check_row[:, 0:chunks], check_row[:, 0:chunks], -1.0, None,
                              ALU.add).then_inc(group_step, 1)
            dve.wait_ge(group_step, 17)
            dve.tensor_reduce(plan_row[:, 1:2], check_row, AX_X, ALU.min).then_inc(group_step, 1)
            dve.wait_ge(group_step, 18)
            dve.tensor_scalar(plan_cell[0:1, 1:2], plan_row[:, 1:2], 0.0, None, ALU.is_ge).then_inc(group_step, 1)
            dve.wait_ge(base_spread, 1)
            dve.wait_ge(turn_out, 2 * blocks)
            by_group = offset[:, :].rearrange("p (g t) -> p g t", t=GROUP)
            dve.tensor_tensor(by_group, by_group,
                              bank[:, 3, 0:groups].rearrange("p (g a) -> p g a", a=1).broadcast_to([P, groups, GROUP]),
                              ALU.subtract).then_inc(group_step, 1)

        def setup_tensor(pe):
            pe.wait_ge(const_ready, 3)
            pe.wait_ge(raw_in, 16 * n_raw)
            for k in range(n_raw):
                pe.transpose(raw_bank(k), raw_w[:, k, :], ident[:, :]).then_inc(raw_turned, 1)
            pe.wait_ge(as_float, 4)
            pe.wait_ge(raw_used, n_raw)
            for n in range(2 * blocks):
                b, k = n // 2, n % 2
                if n >= 4:
                    pe.wait_ge(turn_out, n - 3)
                pe.transpose(bank[:, 4 + n % 4, 0:P], turn_from[k][:, b, :], ident[:, :]).then_inc(turned, 1)
            pe.wait_ge(ext_made, 2)
            pe.wait_ge(turn_out, 2 * blocks)
            for n in range(2 * blocks):
                b, k = n // 2, n % 2
                if n >= 4:
                    pe.wait_ge(ext_out, n - 3)
                pe.transpose(bank[0:1, 4 + n % 4, 0:P], extremes[:, k, b:b + 1], ident[:, :]).then_inc(ext_turned, 1)
            pe.wait_ge(group_step, 2)
            pe.matmul(bank[:, 3, 0:groups], ones[0:1, :], group_row[0:1, 0, :], start=True,
                      stop=True).then_inc(base_spread, 1)



        def turn_tensor(pe, turn, degrees):
            for g in range(TURN_GROUPS):
                pe.wait_ge(onehot_ready, turn * TURN_GROUPS + g + 1)
                pe.wait_ge(sums_added, turn * TURN_GROUPS + g + 1)
                if degrees:
                    for t in range(GROUP):
                        pe.matmul(bank[:, g % 2, WINDOW:2 * WINDOW], ones[:, :], onehot[:, g % 2, t, :],
                                  start=(t == 0), stop=(t == GROUP - 1))
                for t in range(GROUP):
                    k = g * GROUP + t
                    pe.wait_ge(row_landed[k], (turn + 1) * 16)
                    mm = pe.matmul(bank[:, g % 2, 0:WINDOW], rows[:, k, :], onehot[:, g % 2, t, :],
                                   start=(t == 0), stop=(t == GROUP - 1))
                mm.then_inc(group_done, 1)

        def turn_vector(dve, turn, i, degrees):
            planes = 2 if degrees else 1
            starts = [dve.snap(dve.value_load(group_rows[32:33, bass.ds(i * TURN_GROUPS + g, 1)],
                                              min_val=0, max_val=nodes)) for g in range(TURN_GROUPS)]

            def make(g):
                dve.wait_ge(group_done, turn * TURN_GROUPS + g + TURN_GROUPS - 1)
                tiles = offset[:, bass.ds((i * TURN_GROUPS + g) * GROUP, GROUP)]
                dve.tensor_tensor(
                    onehot[:, g % 2, :, :],
                    tiles.rearrange("p (t a) -> p t a", a=1).broadcast_to([P, GROUP, WINDOW]),
                    window_iota[:, :].rearrange("p (a w) -> p a w", a=1).broadcast_to([P, GROUP, WINDOW]),
                    ALU.is_equal).then_inc(onehot_ready, 1)

            def add(g):
                dve.wait_ge(group_done, turn * TURN_GROUPS + g + TURN_GROUPS + 1)
                dve.wait_ge(sums_added, turn * TURN_GROUPS + g + 2)
                to = sums[:, 0:planes, bass.ds(starts[g], WINDOW)]
                dve.tensor_tensor(to, to, bank[:, g % 2, 0:planes * WINDOW].rearrange(
                    "p (a w) -> p a w", a=planes), ALU.add).then_inc(sums_added, 1)

            for g in range(TURN_GROUPS):
                make(g)
                if g >= 1:
                    add(g - 1)
            add(TURN_GROUPS - 1)

        def first_windows(dve):
            dve.tensor_copy(window_iota[:, :], window_iota0[:, :])
            dve.tensor_scalar(window_row, base_row, float(nodes), None, ALU.min).then_inc(windows_set, 1)

        def edge_pool(pool, number, rounds):

            def hand(i, h, u):
                pool.tensor_copy(idx_ring[:, u, h * HALF:(h + 1) * HALF],
                                 idx[:, bass.ds(i * SLOTS + h * HALF, HALF)]).then_inc(idx_ready, 1)

            with pool.Fori(0, rounds) as r:
                with pool.Fori(0, turns // 2) as pair:
                    for u in range(2):
                        turn = pool.snap((rounds * number + r) * turns + pair * 2 + u)
                        for g in range(TURN_GROUPS):
                            gate(pool, (group_done, turn * TURN_GROUPS + g + 1))
                            if g == 0:
                                hand(pair * 2 + u, 0, u)
                                hand(pair * 2 + u, 1, u)
                            if g % (TURN_GROUPS // 2) == 0:
                                gate(pool, (idx_ready, turn * 2 + g // (TURN_GROUPS // 2) + 1))
                            for k in range(g * GROUP, (g + 1) * GROUP):
                                pool.indirect_dma_start(
                                    rows[:, k, :], None, gathered[number],
                                    bass.IndirectOffsetOnAxis(ap=idx_ring[:, u, k:k + 1], axis=0)).then_inc(row_landed[k], 16)

        def edge_rounds(engine, eng, number, rounds):
            if engine == "pool":
                edge_pool(eng, number, rounds)
            elif engine == "tensor":
                with eng.Fori(0, rounds) as r:
                    with eng.Fori(0, turns) as i:
                        turn_tensor(eng, eng.snap((rounds * number + r) * turns + i), number == 0)
            elif engine == "vector":
                first_windows(eng)
                with eng.Fori(0, rounds) as r:
                    gate(eng, (windows_set, rounds * number + r + number + 1))
                    with eng.Fori(0, turns) as i:
                        turn_vector(eng, eng.snap((rounds * number + r) * turns + i), i, number == 0)
                    eng.wait_ge(onehot_ready, (rounds * number + r) * (turns * TURN_GROUPS) + turns * TURN_GROUPS)
                    eng.tensor_scalar(window_iota[:, :], window_iota[:, :], float(WINDOW), None, ALU.add)
                    eng.tensor_scalar(window_row, window_row, float(WINDOW), float(nodes), ALU.add,
                                      ALU.min).then_inc(windows_set, 1)

        def edge_stage(engine, eng, number):
            def stage(c, q):
                def load(k):
                    return eng.snap(eng.value_load(group_rows[64:65, bass.ds(k, 1)], min_val=0, max_val=turns))
                until = load(c + 1)
                with eng.Fori(load(c), until) as i:
                    turn = eng.snap(number * turns + i)
                    if engine == "tensor":
                        turn_tensor(eng, turn, number == 0)
                    else:
                        turn_vector(eng, turn, i, number == 0)
                eng.wait_ge(sums_added, (number * turns + until) * TURN_GROUPS + 2)
            return stage


        def phase_sems(tag, names):
            return {name: sem(f"{tag}_{name}") for name in names}

        def type_rows_tensor(pe, ph, layer):
            def stage(c, q):
                pe.wait_ge(ph["left_ready"], c + 1)
                for j, at, n in tiles_of(c):
                    for h, copied in enumerate((ph["type_out_v"], ph["type_out_s"])):
                        if j >= 1 or not isinstance(c, int) or c >= 1:
                            pe.wait_ge(copied, c * TILES + j)
                        pe.matmul(bank[0:n, 6 + h, :], left[:, q, at:at + n], edge_wt[:, layer, h * CHUNK:(h + 1) * CHUNK],
                                  start=True, stop=True).then_inc(ph["type_made"], 1)
            return stage

        def type_rows_copy(eng, ph, half):
            def stage(c, q):
                for j, at, n in tiles_of(c):
                    u = j % 2
                    eng.wait_ge(ph["type_made"], (c * TILES + j) * 2 + half + 1)
                    if j >= 2 or not isinstance(c, int) or c >= 1:
                        eng.wait_ge(ph["type_stored"][u], (c * 2 + j // 2) * 16)
                    copy = eng.copy if half else eng.tensor_copy
                    copy(wide[0:n, u, half * CHUNK:(half + 1) * CHUNK],
                         bank[0:n, 6 + half, :]).then_inc(ph["type_out_s"] if half else ph["type_out_v"], 1)
            return stage

        def type_rows_store(sp, ph, table):
            def stage(c, q):
                for j, at, n in tiles_of(c):
                    gate(sp, (ph["type_out_v"], c * TILES + j + 1), (ph["type_out_s"], c * TILES + j + 1))
                    sp.dma_start(table[bass.ds(c * CHUNK + at, n), :],
                                 wide[0:n, j % 2, :]).then_inc(ph["type_stored"][j % 2], 16)
            return stage

        def type_rows_end(sp, ph):
            for u in range(2):
                stored = full_chunks * 2 + len([j for j in range(tail_tiles) if j % 2 == u])
                sp.wait_ge(ph["type_stored"][u], 16 * stored)

        project = phase_sems("project", ["x_turned", "xt_ready", "projected", "left_ready", "type_made",
                                         "type_out_v", "type_out_s"])

        def pair_sems(ph, tag, names):
            for name in names:
                ph[name] = [sem(f"{tag}_{name}{u}") for u in range(2)]
            return ph

        pair_sems(project, "project", ["x_in", "type_stored", "state_stored"])

        def wait_chunk(eng, ph, c, q):
            eng.wait_ge(ph["x_in"][q], 16 * moves(c, q) if isinstance(c, int) else (c - q) * 8 + 16)

        def buffer_stored(eng, semaphores, c, q):
            if not isinstance(c, int) or c >= 2:
                eng.wait_ge(semaphores[q], (c - q) * 8)

        def store_state(sp, ph, ready, buf):
            def stage(c, q):
                gate(sp, (ph[ready], c + 1))
                sp.dma_start(state_dram[:, cols(c)], buf[:, q, 0:width(c)]).then_inc(ph["state_stored"][q], 16)
            return stage

        def load_state(sp, ph, used):
            def stage(c, q):
                if not isinstance(c, int) or c >= 2:
                    gate(sp, (ph[used], c - 1))
                sp.dma_start(state_in[:, q, 0:width(c)], state_dram[:, cols(c)]).then_inc(ph["state_loaded"][q], 16)
            return stage

        def state_stores_end(sp, ph):
            for u in range(2):
                sp.wait_ge(ph["state_stored"][u], 16 * len(range(u, chunks, 2)))

        def left_free(eng, ph, c, q):
            if not isinstance(c, int) or c >= 2:
                eng.wait_ge(ph["type_made"], (c - 1) * (TILES * 2))
            buffer_stored(eng, ph["state_stored"], c, q)

        def nothing():
            pass

        def project_phase(engine, eng):
            ph = project
            if engine == "sync":
                def load(c, q):
                    if not isinstance(c, int) or c >= 2:
                        gate(eng, (ph["x_turned"], c - 1))
                    move_rows(eng, c, x, node_in[:, q], True, ph["x_in"][q])

                def end():
                    type_rows_end(eng, ph)
                    state_stores_end(eng, ph)
                return [(load, 0), (store_state(eng, ph, "left_ready", left), 1), (type_rows_store(eng, ph, type_tables[0]), 2)], end
            if engine == "tensor":
                def turn(c, q):
                    wait_chunk(eng, ph, c, q)
                    reuse(eng, ph["xt_ready"], c)
                    for j, at, n in tiles_of(c):
                        mm = eng.transpose(bank[:, 2, at:at + n], node_in[0:n, q, j, :], ident[0:n, 0:n])
                    mm.then_inc(ph["x_turned"], 1)

                def proj(c, q):
                    n = width(c)
                    eng.wait_ge(ph["xt_ready"], c + 1)
                    reuse(eng, ph["left_ready"], c)
                    eng.matmul(bank[:, 3, 0:n], proj_wt[:, :], tmp[:, q, 0:n], start=True,
                               stop=True).then_inc(ph["projected"], 1)
                return [(turn, 0), (proj, 1), (type_rows_tensor(eng, ph, 0), 2)], nothing
            if engine == "vector":
                def keep(c, q):
                    n = width(c)
                    eng.wait_ge(ph["x_turned"], c + 1)
                    reuse(eng, ph["projected"], c, 2)
                    eng.tensor_copy(tmp[:, q, 0:n], bank[:, 2, 0:n]).then_inc(ph["xt_ready"], 1)
                return [(keep, 0), (type_rows_copy(eng, ph, 0), 2)], nothing
            if engine == "scalar":
                def relu(c, q):
                    n = width(c)
                    eng.wait_ge(ph["projected"], c + 1)
                    left_free(eng, ph, c, q)
                    eng.activation(left[:, q, 0:n], bank[:, 3, 0:n], ACT.Relu,
                                   bias=proj_bias[:, 0:1]).then_inc(ph["left_ready"], 1)
                return [(relu, 1), (type_rows_copy(eng, ph, 1), 2)], nothing

            def end():
                eng.memset(sums[:, 0, :], 0.0)
                eng.memset(sums[:, 1, :], 1.0)
            return [], end

        def gru_tensor(pe, ph, layer):
            def stage(c, q):
                n = width(c)
                reuse(pe, ph["gates_free"], c)
                pe.wait_ge(ph["state_loaded"][q], (c - q) * 8 + 16)
                into = ((2, ((0, 0), (1, 0))), (3, ((0, 1), (1, 1))), (4, ((0, 2),)), (5, ((1, 2),)))
                for b, terms in into:
                    for k, (side, g) in enumerate(terms):
                        moving = state_in[:, q, 0:n] if side else sums[:, 0, cols(c)]
                        mm = pe.matmul(bank[:, b, 0:n], gru_wt[:, layer, side, g * P:(g + 1) * P], moving,
                                       start=(k == 0), stop=(k == len(terms) - 1))
                mm.then_inc(ph["gates_made"], 1)
            return stage

        def gru_scalar_gates(act, ph, layer):
            def stage(c, q):
                n = width(c)
                act.wait_ge(ph["gates_made"], c + 1)
                reuse(act, ph["blended"], c)
                for g in range(2):
                    act.activation(tmp[:, g, 0:n], bank[:, 2 + g, 0:n], ACT.Sigmoid,
                                   bias=rz_bias[:, layer, g:g + 1]).then_inc(ph["rz_ready"], 1)
            return stage

        def gru_vector_candidate(dve, ph, layer):
            def stage(c, q):
                n = width(c)
                dve.wait_ge(ph["rz_ready"], c * 2 + 1)
                reuse(dve, ph["blended"], c)
                dve.scalar_tensor_tensor(out=tmp[:, 2, 0:n], in0=bank[:, 5, 0:n],
                                         scalar=gate_bias[:, layer, 1, 2:3], in1=tmp[:, 0, 0:n],
                                         op0=ALU.add, op1=ALU.mult).then_inc(ph["cand_step"], 1)
                dve.wait_ge(ph["rz_ready"], c * 2 + 2)
                dve.wait_ge(ph["cand_step"], c + 1)
                dve.tensor_tensor(tmp[:, 2, 0:n], tmp[:, 2, 0:n], bank[:, 4, 0:n], ALU.add).then_inc(ph["gates_free"], 1)
            return stage

        def gru_scalar_tanh(act, ph, layer):
            def stage(c, q):
                n = width(c)
                act.wait_ge(ph["gates_free"], c + 1)
                act.activation(tmp[:, 3, 0:n], tmp[:, 2, 0:n], ACT.Tanh,
                               bias=gate_bias[:, layer, 0, 2:3]).then_inc(ph["cand_ready"], 1)
            return stage

        def gru_vector_blend(dve, ph, wait_left):
            def stage(c, q):
                n = width(c)
                dve.wait_ge(ph["cand_ready"], c + 1)
                wait_left(c, q)
                dve.tensor_tensor(tmp[:, 2, 0:n], state_in[:, q, 0:n], tmp[:, 3, 0:n],
                                  ALU.subtract).then_inc(ph["blend_step"], 1)
                dve.wait_ge(ph["blend_step"], c * 3 + 1)
                dve.tensor_tensor(tmp[:, 2, 0:n], tmp[:, 2, 0:n], tmp[:, 1, 0:n], ALU.mult).then_inc(ph["blend_step"], 1)
                dve.wait_ge(ph["blend_step"], c * 3 + 2)
                dve.tensor_tensor(tmp[:, 2, 0:n], tmp[:, 2, 0:n], tmp[:, 3, 0:n], ALU.add).then_inc(ph["blend_step"], 1)
                dve.wait_ge(ph["blend_step"], c * 3 + 3)
                dve.tensor_scalar(left[:, q, 0:n], tmp[:, 2, 0:n], 0.0, None, ALU.max).then_inc(ph["blended"], 1)
            return stage

        def gru_phase(tag, names):
            ph = phase_sems(tag, ["gates_made", "gates_free", "rz_ready", "cand_step", "cand_ready", "blend_step",
                                  "blended"] + names)
            ph["left_ready"] = ph["blended"]
            return pair_sems(ph, tag, ["state_loaded", "state_stored"])

        update1 = gru_phase("update1", ["type_made", "type_out_v", "type_out_s"])
        pair_sems(update1, "update1", ["type_stored"])

        def update1_phase(engine, eng):
            ph = update1
            if engine == "sync":
                def end():
                    type_rows_end(eng, ph)
                    state_stores_end(eng, ph)
                return [(load_state(eng, ph, "blended"), 0), (store_state(eng, ph, "blended", left), 1),
                        (type_rows_store(eng, ph, type_tables[1]), 1)], end
            if engine == "tensor":
                return [(gru_tensor(eng, ph, 0), 0), (type_rows_tensor(eng, ph, 1), 1)], nothing
            if engine == "scalar":
                return [(gru_scalar_gates(eng, ph, 0), 0), (gru_scalar_tanh(eng, ph, 0), 0),
                        (type_rows_copy(eng, ph, 1), 1)], nothing
            if engine == "vector":
                def clear(c, q):
                    n = width(c)
                    eng.tensor_copy(sums[:, 0, cols(c)], zero[:, 0:1].broadcast_to([P, n]))

                def end():
                    eng.memset(sums[:, 0, nodes:sums_width], 0.0)
                return [(gru_vector_candidate(eng, ph, 0), 0),
                        (gru_vector_blend(eng, ph, lambda c, q: left_free(eng, ph, c, q)), 0),
                        (type_rows_copy(eng, ph, 0), 1), (clear, 0)], end
            return [], nothing

        def conv_rows_tensor(pe, ph, w, buf, wait_banks=None):
            def stage(c, q):
                n = width(c)
                pe.wait_ge(ph["scaled"], c + 1)
                reuse(pe, ph["table_out"], c)
                if wait_banks:
                    wait_banks(c)
                for j, at, m in tiles_of(c):
                    mm = pe.matmul(bank[0:m, 6, j * P:(j + 1) * P], buf(q)[:, at:at + m], conv_w[:, w, :],
                                   start=True, stop=True)
                mm.then_inc(ph["table_made"], 1)
                reuse(pe, ph["loops_out"], c)
                pe.matmul(bank[:, 7, 0:n], conv_w[:, w, :], buf(q)[:, 0:n], start=True,
                          stop=True).then_inc(ph["loops_made"], 1)
            return stage

        def conv_rows_scalar(act, ph):
            def stage(c, q):
                n = width(c)
                act.wait_ge(ph["table_made"], c + 1)
                if not isinstance(c, int) or c >= 2:
                    act.wait_ge(ph["table_stored"][q], (c - q) * 8)
                for m, j0, j1 in [(P, 0, TILES)] if n == CHUNK else [(m, j, j + 1) for j, _, m in tiles_of(c)]:
                    op = act.copy(wide[0:m, q, j0 * P:j1 * P], bank[0:m, 6, j0 * P:j1 * P])
                op.then_inc(ph["table_out"], 1)
                act.wait_ge(ph["loops_made"], c + 1)
                act.copy(sums[:, 0, cols(c)], bank[:, 7, 0:n]).then_inc(ph["loops_out"], 1)
            return stage

        def conv_rows_store(sp, ph, table):
            def stage(c, q):
                gate(sp, (ph["table_out"], c + 1))
                move_rows(sp, c, table, wide[:, q, 0:CHUNK].rearrange("p (j d) -> p j d", d=P), False,
                          ph["table_stored"][q])
            return stage

        def stores_end(sp, sems):
            for u in range(2):
                sp.wait_ge(sems[u], 16 * moves(chunks - 1, u))

        def norm_vector(dve, ph, b):
            def stage(c, q):
                tiles = tiles_of(c)
                wait_chunk(dve, ph, c, q)
                dve.wait_ge(ph["rows_made"], c + 1)
                spans = [(P, 0, TILES)] if width(c) == CHUNK else [(m, j, j + 1) for j, _, m in tiles]
                for m, j0, j1 in spans:
                    r = node_in[0:m, q, j0:j1, :]
                    op = dve.tensor_tensor(r, r, bank[0:m, b, j0 * P:j1 * P].rearrange("p (j d) -> p j d", d=P), ALU.add)
                op.then_inc(ph["norm_step"], 1)
                dve.wait_ge(ph["norm_step"], c * 3 + 1)
                for j, _, m in tiles:
                    op = dve.bn_stats(stat[0:m, j, :], node_in[0:m, q, j, :])
                op.then_inc(ph["norm_step"], 1)
                gate(dve, (ph["norm_step"], c * 3 + 2))
                for j, _, m in tiles:
                    op = dve.bn_aggr(moments[0:m, j, :], stat[0:m, j, :])
                op.then_inc(ph["norm_step"], 1)
                dve.wait_ge(ph["rstd_ready"], c * 2 + 1)
                for m, j0, j1 in spans:
                    op = dve.reciprocal(rstd[0:m, j0:j1], rstd[0:m, j0:j1])
                op.then_inc(ph["rstd_ready"], 1)
                dve.wait_ge(ph["rstd_ready"], c * 2 + 2)
                for j, _, m in tiles:
                    op = dve.tensor_scalar(node_in[0:m, q, j, :], node_in[0:m, q, j, :], moments[0:m, j, 0:1],
                                           rstd[0:m, j:j + 1], ALU.subtract, ALU.mult)
                op.then_inc(ph["normed"], 1)
            return stage

        def norm_scalar(act, ph):
            def stage(c, q):
                act.wait_ge(ph["norm_step"], c * 3 + 3)
                for m, j0, j1 in [(P, 0, TILES)] if width(c) == CHUNK else [(m, j, j + 1) for j, _, m in tiles_of(c)]:
                    op = act.activation(rstd[0:m, j0:j1], moments[0:m, j0:j1, 1], ACT.Sqrt, bias=eps[0:m, 0:1])
                op.then_inc(ph["rstd_ready"], 1)
            return stage

        def normed_store(sp, ph, table):
            def stage(c, q):
                gate(sp, (ph["normed"], c + 1))
                move_rows(sp, c, table, node_in[:, q], False, ph["normed_stored"][q])
            return stage

        def load_again(sp, ph, table):
            def stage(c, q):
                if not isinstance(c, int) or c >= 2:
                    turned_too = [(ph["normed_turned"], c - 1)] if ph is update2 else []
                    gate(sp, (ph["normed_stored"][q], (c - q) * 8), *turned_too)
                move_rows(sp, c, table, node_in[:, q], True, ph["x_in"][q])
            return stage

        def out_rows_tensor(pe, ph, b, w, bias, lag_sem, wait_bank=None):
            def stage(c, q):
                pe.wait_ge(lag_sem, c + 1)
                if not isinstance(c, int) or c >= 1:
                    pe.wait_ge(ph["norm_step"], (c - 1) * 3 + 1)
                if wait_bank:
                    wait_bank(c)
                for j, at, m in tiles_of(c):
                    pe.matmul(bank[0:m, b, j * P:(j + 1) * P], left[:, q, at:at + m], w, start=True, stop=False)
                    mm = pe.matmul(bank[0:m, b, j * P:(j + 1) * P], ones[0:1, 0:m], bias, start=False, stop=True)
                mm.then_inc(ph["rows_made"], 1)
            return stage

        update2 = gru_phase("update2", ["rows_made", "norm_step", "rstd_ready", "normed", "normed_turned", "scaled",
                                        "kept", "table_made", "table_out", "loops_made", "loops_out", "inverted",
                                        "dinv_ready"])
        pair_sems(update2, "update2", ["x_in", "normed_stored", "table_stored"])

        def scaled_buf(q):
            return wide[:, q, CHUNK:2 * CHUNK]

        def update2_phase(engine, eng):
            ph = update2
            if engine == "sync":
                def end():
                    stores_end(eng, ph["normed_stored"])
                    stores_end(eng, ph["table_stored"])
                    state_stores_end(eng, ph)
                return [(load_state(eng, ph, "blended"), 0), (load_again(eng, ph, x), 0),
                        (normed_store(eng, ph, x1_dram), 1), (store_state(eng, ph, "kept", state_out), 2),
                        (conv_rows_store(eng, ph, conv_tables[0]), 3)], end
            if engine == "tensor":
                def rows_bank(c):
                    if not isinstance(c, int) or c >= 3:
                        eng.wait_ge(ph["table_out"], c - 2)

                def turn(c, q):
                    eng.wait_ge(ph["normed"], c + 1)
                    reuse(eng, ph["kept"], c)
                    if not isinstance(c, int) or c >= 2:
                        eng.wait_ge(ph["loops_out"], c - 1)
                    for j, at, m in tiles_of(c):
                        mm = eng.transpose(bank[:, 7, at:at + m], node_in[0:m, q, j, :], ident[0:m, 0:m])
                    mm.then_inc(ph["normed_turned"], 1)

                def conv_banks(c):
                    later = min(c + 3, chunks) if isinstance(c, int) else c + 3
                    eng.wait_ge(ph["norm_step"], (later - 1) * 3 + 1)
                    later = min(c + 2, chunks) if isinstance(c, int) else c + 2
                    eng.wait_ge(ph["kept"], later)
                return [(gru_tensor(eng, ph, 1), 0),
                        (out_rows_tensor(eng, ph, 6, out_wt[:, :], bias_rows[0:1, 0, :], ph["blended"], rows_bank), 1),
                        (turn, 2), (conv_rows_tensor(eng, ph, 0, scaled_buf, conv_banks), 3)], nothing
            if engine == "scalar":
                def dinv(c, q):
                    eng.wait_ge(ph["inverted"], c + 1)
                    eng.activation(sums[:, 1, cols(c)], sums[:, 1, cols(c)], ACT.Sqrt).then_inc(ph["dinv_ready"], 1)

                def keep(c, q):
                    n = width(c)
                    eng.wait_ge(ph["scaled"], c + 1)
                    buffer_stored(eng, ph["state_stored"], c, q)
                    eng.copy(state_out[:, q, 0:n], bank[:, 7, 0:n]).then_inc(ph["kept"], 1)
                return [(gru_scalar_gates(eng, ph, 1), 0), (gru_scalar_tanh(eng, ph, 1), 0), (dinv, 1),
                        (norm_scalar(eng, ph), 1), (keep, 2), (conv_rows_scalar(eng, ph), 3)], nothing
            if engine == "vector":
                def invert(c, q):
                    eng.reciprocal(sums[:, 1, cols(c)], sums[:, 1, cols(c)]).then_inc(ph["inverted"], 1)

                def scale(c, q):
                    n = width(c)
                    eng.wait_ge(ph["normed_turned"], c + 1)
                    eng.wait_ge(ph["dinv_ready"], c + 1)
                    reuse(eng, ph["loops_made"], c, 2)
                    eng.tensor_tensor(scaled_buf(q)[:, 0:n], bank[:, 7, 0:n], sums[:, 1, cols(c)],
                                      ALU.mult).then_inc(ph["scaled"], 1)

                def end():
                    eng.tensor_single_scalar(idx[:, :], idx[:, :], types_log2, ALU.logical_shift_right)
                blend = gru_vector_blend(eng, ph, lambda c, q: reuse(eng, ph["rows_made"], c, 2))
                return [(scale, 2), (gru_vector_candidate(eng, ph, 1), 0), (blend, 0), (norm_vector(eng, ph, 6), 1),
                        (invert, 0)], end
            return [], nothing

        def conv_phase_sems(tag):
            ph = phase_sems(tag, ["root_made", "conv_step", "kept", "scaled", "table_made", "table_out",
                                  "loops_made", "loops_out"])
            return pair_sems(ph, tag, ["table_stored", "state_loaded", "state_stored"])

        convs = [conv_phase_sems("conv1"), conv_phase_sems("conv2")]

        def conv_phase(engine, eng, k):
            ph, root, nxt = convs[k], 2 * k + 1, 2 * k + 2
            keeps = k == 0
            if engine == "sync":
                def end():
                    stores_end(eng, ph["table_stored"])
                    if keeps:
                        state_stores_end(eng, ph)
                keep = [(store_state(eng, ph, "kept", state_out), 1)] if keeps else []
                return [(load_state(eng, ph, "root_made"), 0)] + keep + [(conv_rows_store(eng, ph, conv_tables[(k + 1) % 2]), 1)], end
            if engine == "tensor":
                def root_term(c, q):
                    n = width(c)
                    reuse(eng, ph["conv_step"], c, 2, per=2)
                    eng.wait_ge(ph["state_loaded"][q], (c - q) * 8 + 16)
                    eng.matmul(bank[:, 2 + q, 0:n], conv_w[:, root, :], state_in[:, q, 0:n], start=True,
                               stop=True).then_inc(ph["root_made"], 1)
                return [(root_term, 0), (conv_rows_tensor(eng, ph, nxt, lambda q: left[:, q]), 1)], nothing
            if engine == "scalar":
                def keep(c, q):
                    n = width(c)
                    eng.wait_ge(ph["conv_step"], c * 2 + 2)
                    buffer_stored(eng, ph["state_stored"], c, q)
                    eng.activation(state_out[:, q, 0:n], tmp[:, q, 0:n], ACT.Relu).then_inc(ph["kept"], 1)
                return ([(keep, 0)] if keeps else []) + [(conv_rows_scalar(eng, ph), 1)], nothing
            if engine == "vector":
                def end(c, q):
                    n = width(c)
                    if keeps:
                        reuse(eng, ph["kept"], c, 2)
                    eng.tensor_tensor(tmp[:, q, 0:n], sums[:, 0, cols(c)], sums[:, 1, cols(c)],
                                      ALU.mult).then_inc(ph["conv_step"], 1)
                    eng.wait_ge(ph["conv_step"], c * 2 + 1)
                    eng.wait_ge(ph["root_made"], c + 1)
                    eng.tensor_tensor(tmp[:, q, 0:n], tmp[:, q, 0:n], bank[:, 2 + q, 0:n],
                                      ALU.add).then_inc(ph["conv_step"], 1)
                    eng.wait_ge(ph["conv_step"], c * 2 + 2)
                    reuse(eng, ph["loops_made"], c, 2)
                    eng.scalar_tensor_tensor(out=left[:, q, 0:n], in0=tmp[:, q, 0:n], scalar=0.0,
                                             in1=sums[:, 1, cols(c)], op0=ALU.max,
                                             op1=ALU.mult).then_inc(ph["scaled"], 1)
                return [(end, 0)], nothing
            return [], nothing

        final = phase_sems("final", ["conv_out", "rows_made", "norm_step", "rstd_ready", "normed"])
        pair_sems(final, "final", ["x_in", "normed_stored"])

        def final_phase(engine, eng):
            ph = final
            if engine == "sync":
                return [(load_again(eng, ph, x1_dram), 0), (normed_store(eng, ph, out), 1)], \
                    lambda: stores_end(eng, ph["normed_stored"])
            if engine == "tensor":
                return [(out_rows_tensor(eng, ph, 6, conv_w[:, 5, :], bias_rows[0:1, 1, :], ph["conv_out"]), 0)], nothing
            if engine == "scalar":
                return [(norm_scalar(eng, ph), 1)], nothing
            if engine == "vector":
                def last_conv(c, q):
                    n = width(c)
                    reuse(eng, ph["rows_made"], c, 2)
                    eng.tensor_tensor(left[:, q, 0:n], sums[:, 0, cols(c)], sums[:, 1, cols(c)],
                                      ALU.mult).then_inc(ph["conv_out"], 1)
                return [(last_conv, 0), (norm_vector(eng, ph, 6), 1)], nothing
            return [], nothing


        phases = [update1_phase, update2_phase, lambda e, eng: conv_phase(e, eng, 0),
                  lambda e, eng: conv_phase(e, eng, 1), final_phase]

        def following(engine, eng):
            for number, phase in enumerate(phases):
                stages, end = phase(engine, eng)
                if engine == "vector":
                    first_windows(eng)
                    eng.wait_ge(windows_set, number + 1)
                if engine in ("tensor", "vector"):
                    stages = [(edge_stage(engine, eng, number), 0)] + stages
                if engine == "pool":
                    edge_pool(eng, number, 1)
                if stages:
                    sweep(eng, stages)
                end()
                if number < len(phases) - 1:
                    barrier(eng, engine)

        def apart(engine, eng):
            rounds = eng.snap(eng.value_load(plan_cell[0:1, 0:1], min_val=1, max_val=nodes // WINDOW + 2))
            for number, phase in enumerate(phases):
                edge_rounds(engine, eng, number, rounds)
                barrier(eng, engine)
                stages, end = phase(engine, eng)
                if stages:
                    sweep(eng, stages)
                end()
                if number < len(phases) - 1:
                    barrier(eng, engine)

        def passes(engine, eng):
            stages, end = project_phase(engine, eng)
            if stages:
                sweep(eng, stages)
            end()
            if engine == "tensor":
                eng.sem_inc(group_done, TURN_GROUPS)
            if engine == "vector":
                eng.sem_inc(sums_added, 2)
            barrier(eng, engine)
            ordered = eng.snap(eng.value_load(plan_cell[0:1, 1:2], min_val=0, max_val=1))
            passed = phases_passed[engine]
            with eng.If_eq(eng.to_reg(ordered), 1):
                following(engine, eng)
            phases_passed[engine] = passed
            with eng.Else():
                apart(engine, eng)

        block = ctx.enter_context(nc.Block())

        @block.sync
        def _(sp):
            setup_sync(sp)
            barrier(sp, "sync")
            passes("sync", sp)

        @block.gpsimd
        def _(pool):
            setup_pool(pool)
            barrier(pool, "pool")
            passes("pool", pool)

        @block.scalar
        def _(act):
            for k, (_, to) in enumerate(raw_blocks):
                act.wait_ge(raw_turned, min(k // 4 * 4 + 4, n_raw))
                act.copy(to, raw_bank(k)).then_inc(raw_used, 1)
            barrier(act, "scalar")
            passes("scalar", act)

        @block.vector
        def _(dve):
            setup_vector(dve)
            barrier(dve, "vector")
            passes("vector", dve)

        @block.tensor
        def _(pe):
            setup_tensor(pe)
            barrier(pe, "tensor")
            passes("tensor", pe)


_INS = ['x', 'src', 'dst', 'edge_type_8', 'L0_gnn_node_proj_w', 'L0_gnn_node_proj_b', 'L0_gnn_edge_W',
        'L0_gnn_gru_wih', 'L0_gnn_gru_whh', 'L0_gnn_gru_bih', 'L0_gnn_gru_bhh', 'L0_gnn_out_w', 'L0_gnn_out_b',
        'L1_gnn_W1', 'L1_gnn_R1', 'L1_gnn_W2', 'L1_gnn_R2', 'L1_gnn_W3', 'L1_gnn_Wh', 'L1_gnn_bh']


def kernel(**inputs):
    import numpy as _np
    import concourse.bacc as _bacc
    from concourse import mybir as _mybir
    from concourse.bass_utils import run_bass_kernel_spmd as _run

    nc = _bacc.Bacc("TRN2", target_bir_lowering=False, num_devices=1)
    arrays, args = {}, []
    for name in _INS:
        a = _np.ascontiguousarray(inputs[name])
        arrays[f"in_{name}"] = a
        args.append(nc.dram_tensor(f"in_{name}", a.shape, _mybir.dt.from_np(a.dtype), kind="ExternalInput").ap())
    shape = tuple(inputs["x"].shape)
    args.append(nc.dram_tensor("out_0", shape, _mybir.dt.float32, kind="ExternalOutput").ap())
    gnn_kernel(nc, *args)
    r = _run(nc, [arrays], core_ids=[0])
    return r.results[0]["out_0"]
```

```python
from contextlib import ExitStack

import concourse.bass as bass
from concourse import mybir
from concourse.alu_op_type import AluOpType as ALU

F32 = mybir.dt.float32
I32 = mybir.dt.int32
BF16 = mybir.dt.bfloat16
ACT = mybir.ActivationFunctionType
AX_X = mybir.AxisListType.X

P = 128

GROUP = 4
WINDOW_LOG2 = 7
WINDOW = 1 << WINDOW_LOG2
SLOTS = 24
TURN_GROUPS = SLOTS // GROUP

CHUNK = 512
TILES = CHUNK // P
WIDE = TILES
EPS = 1e-5


def gnn_kernel(nc, x, src, dst, edge_type, proj_w, proj_b, edge_w, gru_wih, gru_whh, gru_bih,
               gru_bhh, out_w, out_b, w1, r1, w2, r2, w3, wh, bh, out):
    nodes, feat = x.shape
    edges = src.shape[0]
    layers, types = edge_w.shape[0], edge_w.shape[1]
    gates = 3
    types_log2 = types.bit_length() - 1
    assert feat == P and types == 1 << types_log2 and types * P == 2 * CHUNK

    full_chunks = nodes // CHUNK
    tail_nodes = nodes - full_chunks * CHUNK
    assert full_chunks % 2 == 0 and 0 < tail_nodes
    chunks = full_chunks + 1
    tail_tiles = -(-tail_nodes // P)

    turns = -(-edges // (P * SLOTS))
    turns += turns % 2
    edge_tiles = turns * SLOTS
    groups = edge_tiles // GROUP
    blocks = -(-edge_tiles // P)
    full_rows = edges // P
    rest_edges = edges - full_rows * P
    used_tiles = full_rows + (rest_edges > 0)
    last_groups = max(1, -(-(used_tiles - (turns - 1) * SLOTS) // GROUP))
    left_out = TURN_GROUPS - last_groups
    sums_width = nodes + WINDOW
    assert groups <= 512

    type_tables = [nc.dram_tensor(f"type_table{u}", (nodes, types * feat), F32, kind="Internal").ap() for u in range(2)]
    conv_tables = [nc.dram_tensor(f"conv_table{u}", (nodes, feat), F32, kind="Internal").ap() for u in range(2)]
    gathered = [t.rearrange("n (t d) -> (n t) d", t=types) for t in type_tables]
    gathered += [conv_tables[0], conv_tables[1], conv_tables[0]]
    state_dram = nc.dram_tensor("state_dram", (P, nodes), F32, kind="Internal").ap()
    x1_dram = nc.dram_tensor("x1_dram", (nodes, feat), F32, kind="Internal").ap()

    with ExitStack() as ctx:
        def sb(name, shape, dt=F32):
            return ctx.enter_context(nc.sbuf_tensor(name, shape, dt))

        def sem(name):
            return ctx.enter_context(nc.semaphore(name))

        sums = sb("sums", [P, 2, sums_width])
        idx = sb("idx", [P, edge_tiles], I32)
        offset = sb("offset", [P, edge_tiles])
        group_rows = sb("group_rows", [P, groups], I32)
        base_row = group_rows[0:1, :]
        window_row = group_rows[32:33, :]
        turn_ends = group_rows[64:65, 0:chunks + 1]
        plan_cell = sb("plan_cell", [1, 4], I32)
        ident = sb("ident", [P, P])
        ones = sb("ones", [P, P])
        ones_bf16 = sb("ones_bf16", [P, P], BF16)
        base_float = sb("base_float", [1, groups])
        zero = sb("zero", [P, 1])
        eps = sb("eps", [P, 1])
        window_iota0 = sb("window_iota0", [P, WINDOW])
        window_iota = sb("window_iota", [P, WINDOW])
        proj_wt = sb("proj_wt", [P, P])
        edge_wt = sb("edge_wt", [P, layers, types * P])
        gru_wt = sb("gru_wt", [P, layers, 2, gates * P])
        out_wt = sb("out_wt", [P, P])
        conv_w = sb("conv_w", [P, 6, P])
        proj_bias = sb("proj_bias", [P, 1])
        gate_bias = sb("gate_bias", [P, layers, 2, gates])
        rz_bias = sb("rz_bias", [P, layers, 2])
        bias_rows = sb("bias_rows", [1, 2, P])

        idx_ring = sb("idx_ring", [P, 2, 2 * SLOTS], I32)
        stat = sb("stat", [P, TILES, 6])
        moments = sb("moments", [P, TILES, 2])
        rstd = sb("rstd", [P, TILES])

        rows = sb("rows", [P, SLOTS, feat])
        onehot = sb("onehot", [P, 2, GROUP, WINDOW])
        onehot_bf16 = onehot[:, :, :, :].rearrange("p u t w -> p (u t w)").bitcast(BF16).rearrange(
            "p (u t w h) -> p u t w h", u=2, t=GROUP, h=2)[:, :, :, :, 1]

        nodes_region = sb("nodes_region", [P, (2 + 2 + 4) * CHUNK + WIDE * types * P])
        node_in = nodes_region[:, 0:2 * CHUNK].rearrange("p (u j d) -> p u j d", u=2, d=P)
        left = nodes_region[:, 2 * CHUNK:4 * CHUNK].rearrange("p (u n) -> p u n", u=2)
        tmp = nodes_region[:, 4 * CHUNK:8 * CHUNK].rearrange("p (u n) -> p u n", u=4)
        wide = nodes_region[:, 8 * CHUNK:8 * CHUNK + WIDE * types * P].rearrange("p (u n) -> p u n", u=WIDE)
        state_in = sb("state_in", [P, 2, CHUNK])
        state_out = sb("state_out", [P, 2, CHUNK])
        n_raw = layers * (types + 2 * gates) + 2
        raw_w = nodes_region[:, 0:n_raw * P].rearrange("p (k d) -> p k d", d=P)

        stage_words = blocks * P
        sums_flat = sums[:, :, :].rearrange("p a n -> p (a n)")
        stage_int = sums_flat[:, 0:3 * stage_words].bitcast(I32).rearrange("p (k b e) -> p k b e", k=3, e=P)
        stage_f = sums_flat[:, 3 * stage_words:6 * stage_words].rearrange("p (k b e) -> p k b e", k=3, e=P)
        stage_dst_f, stage_src_f, stage_type_f = stage_f[:, 0], stage_f[:, 1], stage_f[:, 2]
        extremes = sums_flat[:, 6 * stage_words:6 * stage_words + 2 * blocks].rearrange("p (k b) -> p k b", k=2)
        at_row = 6 * stage_words + 2 * blocks

        def row_part(words):
            nonlocal at_row
            at_row += words
            assert at_row <= 2 * sums_width
            return sums_flat[0:1, at_row - words:at_row]

        ext_row = row_part(2 * stage_words).rearrange("p (k n) -> p k n", k=2)
        group_row = row_part(2 * groups).rearrange("p (k n) -> p k n", k=2)
        turn_row = row_part(turns)
        before_row = row_part(chunks * turns).rearrange("p (c i) -> p c i", c=chunks)
        chunk_end_row = row_part(chunks)
        end_row = row_part(chunks + 1)
        check_row = row_part(chunks + turns)
        plan_row = row_part(8)

        bank = ctx.enter_context(nc.psum_tensor("bank", [P, 8, 512], F32))

        staged_zero = sem("staged_zero")
        edges_in = sem("edges_in")
        weights_in = sem("weights_in")
        bias_in = sem("bias_in")
        raw_in = sem("raw_in")
        raw_turned = sem("raw_turned")
        raw_used = sem("raw_used")
        ident_zero = sem("ident_zero")
        const_ready = sem("const_ready")
        as_float = sem("as_float")
        turned = sem("turned")
        turn_out = sem("turn_out")
        ext_made = sem("ext_made")
        ext_turned = sem("ext_turned")
        ext_out = sem("ext_out")
        group_step = sem("group_step")
        base_kept = sem("base_kept")
        base_spread = sem("base_spread")
        phase_done = sem("phase_done")

        group_done = sem("group_done")
        idx_ready = sem("idx_ready")
        onehot_ready = sem("onehot_ready")
        sums_added = sem("sums_added")
        windows_set = sem("windows_set")
        gate_passed = sem("gate_passed")
        row_landed = [sem(f"row_landed_{k}") for k in range(SLOTS)]

        phases_passed = {}

        def barrier(eng, name):
            n = phases_passed.get(name, 0) + 1
            phases_passed[name] = n
            eng.drain().then_inc(phase_done, 1)
            eng.wait_ge(phase_done, 5 * n)

        def gate(eng, *waits):
            for semaphore, count in waits:
                eng.wait_ge(semaphore, count)
                eng.sem_inc(gate_passed, 1)

        def width(c):
            return tail_nodes if isinstance(c, int) and c == full_chunks else CHUNK

        def tiles_of(c):
            n = width(c)
            return [(j, j * P, min(P, n - j * P)) for j in range(-(-n // P))]

        def cols(c):
            return bass.ds(c * CHUNK, width(c))

        def sweep(eng, stages):
            most = max(lag for _, lag in stages)
            first = most + 2 + most % 2
            for s in range(first):
                for stage, lag in stages:
                    if s - lag >= 0:
                        stage(s - lag, (s - lag) % 2)
            with eng.Fori(first // 2, full_chunks // 2) as pair:
                for u in range(2):
                    for stage, lag in stages:
                        stage(pair * 2 + (u - lag), (u - lag) % 2)
            for s in range(full_chunks, chunks + most):
                for stage, lag in stages:
                    if s - lag < chunks:
                        stage(s - lag, (s - lag) % 2)

        def reuse(eng, semaphore, c, depth=1, per=1):
            if not isinstance(c, int) or c >= depth:
                eng.wait_ge(semaphore, (c - depth) * per + per)

        def move_rows(eng, c, table, buf, load, semaphore):
            if width(c) == CHUNK:
                d = table[bass.ds(c * CHUNK, CHUNK), :].rearrange("(j p) d -> p j d", p=P)
                eng.dma_start(buf if load else d, d if load else buf).then_inc(semaphore, 16)
                return
            for j, at, n in tiles_of(c):
                d = table[c * CHUNK + at:c * CHUNK + at + n, :]
                buf_j = buf[0:n, j, :]
                eng.dma_start(buf_j if load else d, d if load else buf_j).then_inc(semaphore, 16)

        def moves(c, q):
            return sum(1 if width(k) == CHUNK else tail_tiles for k in range(q, c + 1, 2))


        conv_ws = [w1, r1, w2, r2, w3, wh]
        raw_blocks = [proj_wt[:, :], out_wt[:, :]]
        raw_loads = [(0, 1, proj_w), (1, 1, out_w)]
        for layer in range(layers):
            raw_loads.append((len(raw_blocks), types, edge_w[layer].rearrange("t o i -> o t i")))
            raw_blocks += [edge_wt[:, layer, t * P:(t + 1) * P] for t in range(types)]
            for k, w in enumerate((gru_wih, gru_whh)):
                raw_loads.append((len(raw_blocks), gates, w[layer].rearrange("(g o) i -> o g i", g=gates)))
                raw_blocks += [gru_wt[:, layer, k, g * P:(g + 1) * P] for g in range(gates)]
        assert len(raw_blocks) == n_raw <= 32

        def raw_bank(k):
            return bank[:, k // 4, (k % 4) * P:(k % 4 + 1) * P]

        last = blocks - 1
        last_full = full_rows - last * P
        assert 0 <= last_full < P and blocks * P >= edge_tiles

        def setup_sync(sp):
            sp.wait_ge(staged_zero, 3)
            for k, a in enumerate((dst, src, edge_type)):
                body = a[0:last * P * P].rearrange("(b p e) -> p b e", p=P, e=P)
                sp.dma_start(stage_int[:, k, 0:last, :], body).then_inc(edges_in, 16)
                if last_full:
                    sp.dma_start(stage_int[0:last_full, k, last, :],
                                 a[last * P * P:full_rows * P].rearrange("(p e) -> p e", e=P)).then_inc(edges_in, 16)
                if rest_edges:
                    sp.dma_start(stage_int[last_full:last_full + 1, k, last, 0:rest_edges],
                                 a[full_rows * P:edges].rearrange("(p e) -> p e", p=1)).then_inc(edges_in, 16)
            for k, n, block_in in raw_loads:
                sp.dma_start(raw_w[:, k:k + n, :] if n > 1 else raw_w[:, k, :], block_in).then_inc(raw_in, 16)
            sp.dma_start(proj_bias[:, :], proj_b.rearrange("(p a) -> p a", a=1)).then_inc(bias_in, 16)
            for k, w in enumerate(conv_ws):
                sp.dma_start(conv_w[:, k, :], w).then_inc(weights_in, 16)
            for layer in range(layers):
                for k, b in enumerate((gru_bih, gru_bhh)):
                    for g in range(gates):
                        sp.dma_start(gate_bias[:, layer, k, g:g + 1],
                                     b[layer, g * P:(g + 1) * P].rearrange("(p a) -> p a", a=1)).then_inc(weights_in, 16)
            for k, b in enumerate((out_b, bh)):
                sp.dma_start(bias_rows[0:1, k, :], b.rearrange("(a n) -> a n", a=1)).then_inc(weights_in, 16)

        n_edge_loads = 3 * (1 + (last_full > 0) + (rest_edges > 0))
        n_weight_loads = len(conv_ws) + layers * 2 * gates + 2

        def setup_pool(pool):
            for k, value in enumerate((nodes, 0, 0)):
                pool.memset(stage_int[:, k, last, :], value).then_inc(staged_zero, 1)
            pool.iota(chunk_end_row, [[CHUNK, chunks]], base=CHUNK, channel_multiplier=0,
                      allow_small_or_imprecise_dtypes=True)
            pool.iota(window_iota0[:, :], [[1, WINDOW]], base=0, channel_multiplier=0,
                      allow_small_or_imprecise_dtypes=True).then_inc(const_ready, 1)
            pool.memset(zero[:, :], 0.0)
            pool.memset(eps[:, :], EPS)
            pool.memset(ones_bf16[:, :], 1.0)
            pool.memset(ones[:, :], 1.0).then_inc(const_ready, 1)
            pool.memset(ident[:, :], 0.0).then_inc(ident_zero, 1)
            pool.wait_ge(ident_zero, 1)
            pool.affine_select(out=ident[:, :], in_=ident[:, :], compare_op=ALU.not_equal, fill=1.0, base=0,
                               pattern=[[-1, P]], channel_multiplier=1).then_inc(const_ready, 1)

        turn_from = [stage_dst_f, stage_type_f]
        turn_to = [offset, idx]

        def block_tiles(b):
            return min(P, edge_tiles - b * P)

        def setup_vector(dve):
            dve.wait_ge(edges_in, 16 * n_edge_loads)
            for k in range(3):
                dve.tensor_copy(stage_f[:, k], stage_int[:, k]).then_inc(as_float, 1)
            dve.wait_ge(as_float, 3)
            dve.scalar_tensor_tensor(out=stage_type_f, in0=stage_src_f, scalar=float(types), in1=stage_type_f,
                                     op0=ALU.mult, op1=ALU.add).then_inc(as_float, 1)
            dve.tensor_reduce(extremes[:, 0, :], stage_dst_f, AX_X, ALU.min).then_inc(ext_made, 1)
            dve.tensor_reduce(extremes[:, 1, :], stage_dst_f, AX_X, ALU.max).then_inc(ext_made, 1)
            for n in range(2 * blocks):
                b, k = n // 2, n % 2
                dve.wait_ge(turned, n + 1)
                dve.tensor_copy(turn_to[k][:, b * P:b * P + block_tiles(b)],
                                bank[:, 4 + n % 4, 0:block_tiles(b)]).then_inc(turn_out, 1)
            for n in range(2 * blocks):
                b, k = n // 2, n % 2
                dve.wait_ge(ext_turned, n + 1)
                dve.tensor_copy(ext_row[:, k, b * P:(b + 1) * P], bank[0:1, 4 + n % 4, 0:P]).then_inc(ext_out, 1)
            dve.wait_ge(ext_out, 2 * blocks)
            for k, op in enumerate((ALU.min, ALU.max)):
                dve.tensor_reduce(group_row[:, k, :],
                                  ext_row[:, k, 0:edge_tiles].rearrange("p (g t) -> p g t", t=GROUP),
                                  AX_X, op).then_inc(group_step, 1)
            dve.wait_ge(group_step, 2)
            dve.tensor_copy(base_row, group_row[:, 0, :]).then_inc(group_step, 1)
            dve.tensor_copy(base_float[:, :], group_row[:, 0, :]).then_inc(base_kept, 1)
            dve.tensor_tensor(group_row[:, 1, :], group_row[:, 1, :], group_row[:, 0, :],
                              ALU.subtract).then_inc(group_step, 1)
            dve.tensor_reduce(turn_row, group_row[:, 0, :].rearrange("p (i g) -> p i g", g=TURN_GROUPS),
                              AX_X, ALU.min).then_inc(group_step, 1)
            dve.wait_ge(group_step, 5)
            dve.tensor_reduce(plan_row[:, 0:1], group_row[:, 1, :], AX_X, ALU.max).then_inc(group_step, 1)
            dve.wait_ge(group_step, 6)
            dve.tensor_copy(plan_cell[0:1, 2:3], plan_row[:, 0:1]).then_inc(group_step, 1)
            dve.wait_ge(group_step, 7)
            dve.tensor_single_scalar(plan_cell[0:1, 3:4], plan_cell[0:1, 2:3], WINDOW_LOG2,
                                     ALU.logical_shift_right).then_inc(group_step, 1)
            dve.wait_ge(group_step, 8)
            dve.tensor_scalar(plan_cell[0:1, 0:1], plan_cell[0:1, 3:4], 1.0, None, ALU.add).then_inc(group_step, 1)
            shape = [1, chunks, turns]
            dve.tensor_tensor(before_row, turn_row.rearrange("p (c i) -> p c i", c=1).broadcast_to(shape),
                              chunk_end_row.rearrange("p (c i) -> p c i", i=1).broadcast_to(shape),
                              ALU.is_lt).then_inc(group_step, 1)
            dve.memset(end_row[:, 0:1], 0.0)
            dve.wait_ge(group_step, 10)
            dve.tensor_reduce(end_row[:, 1:chunks + 1], before_row, AX_X, ALU.add).then_inc(group_step, 1)
            dve.wait_ge(group_step, 11)
            dve.memset(end_row[:, chunks:chunks + 1], float(turns)).then_inc(group_step, 1)
            dve.wait_ge(group_step, 12)
            dve.tensor_copy(turn_ends, end_row).then_inc(group_step, 1)
            dve.tensor_tensor(check_row[:, 0:chunks], end_row[:, 1:chunks + 1], end_row[:, 0:chunks],
                              ALU.subtract).then_inc(group_step, 1)
            dve.tensor_tensor(check_row[:, chunks:chunks + turns - 1], turn_row[:, 1:turns],
                              turn_row[:, 0:turns - 1], ALU.subtract).then_inc(group_step, 1)
            dve.tensor_scalar(check_row[:, chunks + turns - 1:chunks + turns], plan_row[:, 0:1], -1.0,
                              float(WINDOW - 1), ALU.mult, ALU.add).then_inc(group_step, 1)
            dve.wait_ge(group_step, 16)
            dve.tensor_scalar(check_row[:, 0:chunks], check_row[:, 0:chunks], -1.0, None,
                              ALU.add).then_inc(group_step, 1)
            dve.wait_ge(group_step, 17)
            dve.tensor_reduce(plan_row[:, 1:2], check_row, AX_X, ALU.min).then_inc(group_step, 1)
            dve.wait_ge(group_step, 18)
            dve.tensor_scalar(plan_cell[0:1, 1:2], plan_row[:, 1:2], 0.0, None, ALU.is_ge).then_inc(group_step, 1)
            dve.wait_ge(weights_in, 16 * n_weight_loads)
            dve.tensor_tensor(rz_bias[:, :, :], gate_bias[:, :, 0, 0:2], gate_bias[:, :, 1, 0:2], ALU.add)
            dve.wait_ge(base_spread, 1)
            dve.wait_ge(turn_out, 2 * blocks)
            by_group = offset[:, :].rearrange("p (g t) -> p g t", t=GROUP)
            dve.tensor_tensor(by_group, by_group,
                              bank[:, 0, 0:groups].rearrange("p (g a) -> p g a", a=1).broadcast_to([P, groups, GROUP]),
                              ALU.subtract).then_inc(group_step, 1)

        def setup_tensor(pe):
            pe.wait_ge(const_ready, 3)
            pe.wait_ge(raw_in, 16 * len(raw_loads))
            for k in range(n_raw):
                pe.transpose(raw_bank(k), raw_w[:, k, :], ident[:, :]).then_inc(raw_turned, 1)
            pe.wait_ge(as_float, 4)
            pe.wait_ge(raw_used, n_raw)
            for n in range(2 * blocks):
                b, k = n // 2, n % 2
                if n >= 4:
                    pe.wait_ge(turn_out, n - 3)
                pe.transpose(bank[:, 4 + n % 4, 0:P], turn_from[k][:, b, :], ident[:, :]).then_inc(turned, 1)
            pe.wait_ge(ext_made, 2)
            pe.wait_ge(turn_out, 2 * blocks)
            for n in range(2 * blocks):
                b, k = n // 2, n % 2
                if n >= 4:
                    pe.wait_ge(ext_out, n - 3)
                pe.transpose(bank[0:1, 4 + n % 4, 0:P], extremes[:, k, b:b + 1], ident[:, :]).then_inc(ext_turned, 1)
            pe.wait_ge(ext_out, 2 * blocks)



        def turn_groups(i):
            if isinstance(i, int) and i == turns - 1:
                return [(g, 1 + (left_out if g == last_groups - 1 else 0)) for g in range(last_groups)]
            return [(g, 1) for g in range(TURN_GROUPS)]

        def turn_tensor(pe, done, i, degrees):
            turn = pe.snap(pe.to_reg(done * turns + i))
            fewer = pe.snap(pe.to_reg(done * (turns - 1) + i)) if left_out else turn
            for g, count in turn_groups(i):
                pe.wait_ge(onehot_ready, turn * TURN_GROUPS + g + 1)
                pe.wait_ge(sums_added, turn * TURN_GROUPS + g + 1)
                if degrees:
                    for t in range(GROUP):
                        pe.matmul(bank[:, g % 2, WINDOW:2 * WINDOW], ones_bf16[:, :], onehot_bf16[:, g % 2, t, :],
                                  start=(t == 0), stop=(t == GROUP - 1))
                for t in range(GROUP):
                    k = g * GROUP + t
                    pe.wait_ge(row_landed[k], ((turn if g < last_groups else fewer) + 1) * 16)
                    mm = pe.matmul(bank[:, g % 2, 0:WINDOW], rows[:, k, :], onehot[:, g % 2, t, :],
                                   start=(t == 0), stop=(t == GROUP - 1))
                mm.then_inc(group_done, count)

        def turn_vector(dve, done, i, degrees):
            turn = dve.snap(dve.to_reg(done * turns + i))
            in_turn = turn_groups(i)
            planes = 2 if degrees else 1
            starts = {}

            def make(g, count):
                dve.wait_ge(group_done, turn * TURN_GROUPS + g + TURN_GROUPS - 1)
                tiles = offset[:, bass.ds((i * TURN_GROUPS + g) * GROUP, GROUP)]
                dve.tensor_tensor(
                    onehot[:, g % 2, :, :],
                    tiles.rearrange("p (t a) -> p t a", a=1).broadcast_to([P, GROUP, WINDOW]),
                    window_iota[:, :].rearrange("p (a w) -> p a w", a=1).broadcast_to([P, GROUP, WINDOW]),
                    ALU.is_equal).then_inc(onehot_ready, count)
                starts[g] = dve.snap(dve.value_load(group_rows[32:33, bass.ds(i * TURN_GROUPS + g, 1)],
                                                    min_val=0, max_val=nodes))

            def add(g, count):
                dve.wait_ge(group_done, turn * TURN_GROUPS + g + TURN_GROUPS + 1)
                dve.wait_ge(sums_added, turn * TURN_GROUPS + g + 2)
                to = sums[:, 0:planes, bass.ds(starts[g], WINDOW)]
                dve.tensor_tensor(to, to, bank[:, g % 2, 0:planes * WINDOW].rearrange(
                    "p (a w) -> p a w", a=planes), ALU.add).then_inc(sums_added, count)

            for g, count in in_turn:
                make(g, count)
                if g >= 1:
                    add(*in_turn[g - 1])
            add(*in_turn[-1])

        def first_windows(dve):
            dve.tensor_copy(window_iota[:, :], window_iota0[:, :])
            dve.tensor_scalar(window_row, base_row, float(nodes), None, ALU.min).then_inc(windows_set, 1)

        def edge_pool(pool, number, rounds):

            def hand(i, v):
                pool.tensor_copy(idx_ring[:, v, :], idx[:, bass.ds(i * SLOTS, 2 * SLOTS)]).then_inc(idx_ready, 1)

            def take_pair(r, n, v):
                i = n * 2
                for u in range(2):
                    turn = pool.snap((rounds * number + r) * turns + i + u)
                    for g, _ in turn_groups(i + u):
                        gate(pool, (group_done, turn * TURN_GROUPS + g + 1))
                        if u == 0 and g == 0:
                            gate(pool, (idx_ready, pool.snap((rounds * number + r) * (turns // 2) + n) + 1))
                        if u == 0 and g == TURN_GROUPS - 1 and not (isinstance(i, int) and i == turns - 2):
                            hand(i + 2, 1 - v)
                        for k in range(g * GROUP, (g + 1) * GROUP):
                            at = u * SLOTS + k
                            pool.indirect_dma_start(
                                rows[:, k, :], None, gathered[number],
                                bass.IndirectOffsetOnAxis(ap=idx_ring[:, v, at:at + 1], axis=0)).then_inc(row_landed[k], 16)

            looped = (turns // 2 - 1) // 2
            with pool.Fori(0, rounds) as r:
                gate(pool, (group_done, pool.snap((rounds * number + r) * turns) * TURN_GROUPS + TURN_GROUPS))
                hand(0, 0)
                with pool.Fori(0, looped) as step:
                    for v in range(2):
                        take_pair(r, step * 2 + v, v)
                for n in range(looped * 2, turns // 2):
                    take_pair(r, n, n % 2)

        def edge_rounds(engine, eng, number, rounds):
            if engine == "pool":
                edge_pool(eng, number, rounds)
            elif engine == "tensor":
                with eng.Fori(0, rounds) as r:
                    done = eng.snap(rounds * number + r)
                    with eng.Fori(0, turns - 1) as i:
                        turn_tensor(eng, done, i, number == 0)
                    turn_tensor(eng, done, turns - 1, number == 0)
            elif engine == "vector":
                first_windows(eng)
                with eng.Fori(0, rounds) as r:
                    gate(eng, (windows_set, rounds * number + r + number + 1))
                    done = eng.snap(rounds * number + r)
                    with eng.Fori(0, turns - 1) as i:
                        turn_vector(eng, done, i, number == 0)
                    turn_vector(eng, done, turns - 1, number == 0)
                    eng.wait_ge(onehot_ready, (rounds * number + r) * (turns * TURN_GROUPS) + turns * TURN_GROUPS)
                    eng.tensor_scalar(window_iota[:, :], window_iota[:, :], float(WINDOW), None, ALU.add)
                    eng.tensor_scalar(window_row, window_row, float(WINDOW), float(nodes), ALU.add,
                                      ALU.min).then_inc(windows_set, 1)

        def edge_stage(engine, eng, number):
            def stage(c, q):
                def load(k):
                    return eng.snap(eng.value_load(group_rows[64:65, bass.ds(k, 1)], min_val=0, max_val=turns))
                run = turn_tensor if engine == "tensor" else turn_vector
                if isinstance(c, int) and c == full_chunks:
                    until, start = turns, load(c)
                    with eng.If_lt(eng.to_reg(start), turns - 1):
                        with eng.Fori(start, turns - 1) as i:
                            run(eng, number, i, number == 0)
                    run(eng, number, turns - 1, number == 0)
                else:
                    until = load(c + 1)
                    with eng.Fori(load(c), until) as i:
                        run(eng, number, i, number == 0)
                eng.wait_ge(sums_added, (number * turns + until) * TURN_GROUPS + 2)
            return stage


        def phase_sems(tag, names):
            return {name: sem(f"{tag}_{name}") for name in names}

        def type_bank(j, half, pairs):
            return (6 if pairs == 1 or j % 2 else 4) + half

        def type_rows_tensor(pe, ph, layer, pairs):
            def stage(c, q):
                pe.wait_ge(ph["left_ready"], c + 1)
                for j, at, n in tiles_of(c):
                    for h, copied in enumerate((ph["type_out_0"], ph["type_out_1"])):
                        if j >= pairs or not isinstance(c, int) or c >= 1:
                            pe.wait_ge(copied, c * TILES + (j - pairs + 1))
                        pe.matmul(bank[0:n, type_bank(j, h, pairs), :], left[:, q, at:at + n], edge_wt[:, layer, h * CHUNK:(h + 1) * CHUNK],
                                  start=True, stop=True).then_inc(ph["type_made"], 1)
            return stage

        def type_rows_copy(act, ph, pairs):
            def stage(c, q):
                for j, at, n in tiles_of(c):
                    if not isinstance(c, int) or c >= 1:
                        act.wait_ge(ph["type_stored"][j], c * 16)
                    for half, out_sem in enumerate((ph["type_out_0"], ph["type_out_1"])):
                        act.wait_ge(ph["type_made"], (c * TILES + j) * 2 + half + 1)
                        act.copy(wide[0:n, j, half * CHUNK:(half + 1) * CHUNK],
                                 bank[0:n, type_bank(j, half, pairs), :]).then_inc(out_sem, 1)
            return stage

        def type_rows_store(sp, ph, table):
            def stage(c, q):
                for j, at, n in tiles_of(c):
                    gate(sp, (ph["type_out_0"], c * TILES + j + 1), (ph["type_out_1"], c * TILES + j + 1))
                    sp.dma_start(table[bass.ds(c * CHUNK + at, n), :],
                                 wide[0:n, j, :]).then_inc(ph["type_stored"][j], 16)
            return stage

        def type_rows_end(sp, ph):
            for j in range(WIDE):
                sp.wait_ge(ph["type_stored"][j], 16 * (full_chunks + (j < tail_tiles)))

        project = phase_sems("project", ["x_turned", "xt_ready", "projected", "left_ready", "type_made",
                                         "type_out_0", "type_out_1"])

        def pair_sems(ph, tag, names, parts=2):
            for name in names:
                ph[name] = [sem(f"{tag}_{name}{u}") for u in range(parts)]
            return ph

        pair_sems(project, "project", ["x_in", "state_stored"])
        pair_sems(project, "project", ["type_stored"], WIDE)

        def wait_chunk(eng, ph, c, q):
            eng.wait_ge(ph["x_in"][q], 16 * moves(c, q) if isinstance(c, int) else (c - q) * 8 + 16)

        def buffer_stored(eng, semaphores, c, q):
            if not isinstance(c, int) or c >= 2:
                eng.wait_ge(semaphores[q], (c - q) * 8)

        def store_state(sp, ph, ready, buf):
            def stage(c, q):
                gate(sp, (ph[ready], c + 1))
                sp.dma_start(state_dram[:, cols(c)], buf[:, q, 0:width(c)]).then_inc(ph["state_stored"][q], 16)
            return stage

        def load_state(sp, ph, used):
            def stage(c, q):
                if not isinstance(c, int) or c >= 2:
                    gate(sp, (ph[used], c - 1))
                sp.dma_start(state_in[:, q, 0:width(c)], state_dram[:, cols(c)]).then_inc(ph["state_loaded"][q], 16)
            return stage

        def state_stores_end(sp, ph):
            for u in range(2):
                sp.wait_ge(ph["state_stored"][u], 16 * len(range(u, chunks, 2)))

        def left_free(eng, ph, c, q):
            if not isinstance(c, int) or c >= 2:
                eng.wait_ge(ph["type_made"], (c - 1) * (TILES * 2))
            buffer_stored(eng, ph["state_stored"], c, q)

        def nothing():
            pass

        def project_phase(engine, eng):
            ph = project
            if engine == "sync":
                def load(c, q):
                    if not isinstance(c, int) or c >= 2:
                        gate(eng, (ph["x_turned"], c - 1))
                    move_rows(eng, c, x, node_in[:, q], True, ph["x_in"][q])

                def end():
                    type_rows_end(eng, ph)
                    state_stores_end(eng, ph)
                return [(load, 0), (store_state(eng, ph, "left_ready", left), 2),
                        (type_rows_store(eng, ph, type_tables[0]), 3)], end
            if engine == "tensor":
                def turn(c, q):
                    wait_chunk(eng, ph, c, q)
                    reuse(eng, ph["xt_ready"], c)
                    for j, at, n in tiles_of(c):
                        mm = eng.transpose(bank[:, 2, at:at + n], node_in[0:n, q, j, :], ident[0:n, 0:n])
                    mm.then_inc(ph["x_turned"], 1)

                def proj(c, q):
                    n = width(c)
                    eng.wait_ge(ph["xt_ready"], c + 1)
                    reuse(eng, ph["left_ready"], c)
                    eng.matmul(bank[:, 3, 0:n], proj_wt[:, :], tmp[:, q, 0:n], start=True,
                               stop=True).then_inc(ph["projected"], 1)
                def end():
                    eng.wait_ge(base_kept, 1)
                    eng.matmul(bank[:, 0, 0:groups], ones[0:1, :], base_float[:, :], start=True,
                               stop=True).then_inc(base_spread, 1)
                return [(turn, 0), (proj, 1), (type_rows_tensor(eng, ph, 0, 2), 2)], end
            if engine == "vector":
                return [], nothing
            if engine == "scalar":
                def keep(c, q):
                    n = width(c)
                    eng.wait_ge(ph["x_turned"], c + 1)
                    reuse(eng, ph["projected"], c, 2)
                    eng.copy(tmp[:, q, 0:n], bank[:, 2, 0:n]).then_inc(ph["xt_ready"], 1)

                def relu(c, q):
                    n = width(c)
                    eng.wait_ge(ph["projected"], c + 1)
                    left_free(eng, ph, c, q)
                    eng.activation(left[:, q, 0:n], bank[:, 3, 0:n], ACT.Relu,
                                   bias=proj_bias[:, 0:1]).then_inc(ph["left_ready"], 1)
                return [(keep, 0), (relu, 1), (type_rows_copy(eng, ph, 2), 2)], nothing

            def end():
                eng.wait_ge(group_step, 19)
                eng.memset(sums[:, 0, :], 0.0)
                eng.memset(sums[:, 1, :], 1.0)
            return [], end

        def gru_tensor(pe, ph, layer):
            def stage(c, q):
                n = width(c)
                reuse(pe, ph["gates_free"], c)
                pe.wait_ge(ph["state_loaded"][q], (c - q) * 8 + 16)
                into = ((2, ((0, 0), (1, 0))), (3, ((0, 1), (1, 1))), (4, ((0, 2),)), (5, ((1, 2),)))
                for b, terms in into:
                    for k, (side, g) in enumerate(terms):
                        moving = state_in[:, q, 0:n] if side else sums[:, 0, cols(c)]
                        mm = pe.matmul(bank[:, b, 0:n], gru_wt[:, layer, side, g * P:(g + 1) * P], moving,
                                       start=(k == 0), stop=(k == len(terms) - 1))
                mm.then_inc(ph["gates_made"], 1)
            return stage

        def gru_scalar_gates(act, ph, layer):
            def stage(c, q):
                n = width(c)
                act.wait_ge(ph["gates_made"], c + 1)
                reuse(act, ph["blended"], c)
                for g in range(2):
                    act.activation(tmp[:, g, 0:n], bank[:, 2 + g, 0:n], ACT.Sigmoid,
                                   bias=rz_bias[:, layer, g:g + 1]).then_inc(ph["rz_ready"], 1)
            return stage

        def gru_vector_candidate(dve, ph, layer):
            def stage(c, q):
                n = width(c)
                dve.wait_ge(ph["rz_ready"], c * 2 + 1)
                reuse(dve, ph["blended"], c)
                dve.scalar_tensor_tensor(out=tmp[:, 2, 0:n], in0=bank[:, 5, 0:n],
                                         scalar=gate_bias[:, layer, 1, 2:3], in1=tmp[:, 0, 0:n],
                                         op0=ALU.add, op1=ALU.mult).then_inc(ph["cand_step"], 1)
                dve.wait_ge(ph["rz_ready"], c * 2 + 2)
                dve.wait_ge(ph["cand_step"], c + 1)
                dve.tensor_tensor(tmp[:, 2, 0:n], tmp[:, 2, 0:n], bank[:, 4, 0:n], ALU.add).then_inc(ph["gates_free"], 1)
            return stage

        def gru_scalar_tanh(act, ph, layer):
            def stage(c, q):
                n = width(c)
                act.wait_ge(ph["gates_free"], c + 1)
                act.activation(tmp[:, 3, 0:n], tmp[:, 2, 0:n], ACT.Tanh,
                               bias=gate_bias[:, layer, 0, 2:3]).then_inc(ph["cand_ready"], 1)
            return stage

        def gru_vector_blend(dve, ph, wait_left):
            def stage(c, q):
                n = width(c)
                dve.wait_ge(ph["cand_ready"], c + 1)
                wait_left(c, q)
                dve.tensor_tensor(tmp[:, 2, 0:n], state_in[:, q, 0:n], tmp[:, 3, 0:n],
                                  ALU.subtract).then_inc(ph["blend_step"], 1)
                dve.wait_ge(ph["blend_step"], c * 3 + 1)
                dve.tensor_tensor(tmp[:, 2, 0:n], tmp[:, 2, 0:n], tmp[:, 1, 0:n], ALU.mult).then_inc(ph["blend_step"], 1)
                dve.wait_ge(ph["blend_step"], c * 3 + 2)
                dve.tensor_tensor(tmp[:, 2, 0:n], tmp[:, 2, 0:n], tmp[:, 3, 0:n], ALU.add).then_inc(ph["blend_step"], 1)
                dve.wait_ge(ph["blend_step"], c * 3 + 3)
                dve.tensor_scalar(left[:, q, 0:n], tmp[:, 2, 0:n], 0.0, None, ALU.max).then_inc(ph["blended"], 1)
            return stage

        def gru_phase(tag, names):
            ph = phase_sems(tag, ["gates_made", "gates_free", "rz_ready", "cand_step", "cand_ready", "blend_step",
                                  "blended"] + names)
            ph["left_ready"] = ph["blended"]
            return pair_sems(ph, tag, ["state_loaded", "state_stored"])

        update1 = gru_phase("update1", ["type_made", "type_out_0", "type_out_1"])
        pair_sems(update1, "update1", ["type_stored"], WIDE)

        def update1_phase(engine, eng):
            ph = update1
            if engine == "sync":
                def end():
                    type_rows_end(eng, ph)
                    state_stores_end(eng, ph)
                return [(load_state(eng, ph, "blended"), 0), (store_state(eng, ph, "blended", left), 1),
                        (type_rows_store(eng, ph, type_tables[1]), 1)], end
            if engine == "tensor":
                return [(gru_tensor(eng, ph, 0), 0), (type_rows_tensor(eng, ph, 1, 1), 1)], nothing
            if engine == "scalar":
                return [(gru_scalar_gates(eng, ph, 0), 0), (gru_scalar_tanh(eng, ph, 0), 0),
                        (type_rows_copy(eng, ph, 1), 1)], nothing
            if engine == "vector":
                def clear(c, q):
                    n = width(c)
                    eng.tensor_copy(sums[:, 0, cols(c)], zero[:, 0:1].broadcast_to([P, n]))

                def end():
                    eng.memset(sums[:, 0, nodes:sums_width], 0.0)
                return [(gru_vector_candidate(eng, ph, 0), 0),
                        (gru_vector_blend(eng, ph, lambda c, q: left_free(eng, ph, c, q)), 0), (clear, 0)], end
            return [], nothing

        def conv_rows_tensor(pe, ph, w, buf, wait_banks=None):
            def stage(c, q):
                n = width(c)
                pe.wait_ge(ph["scaled"], c + 1)
                reuse(pe, ph["table_out"], c)
                if wait_banks:
                    wait_banks(c)
                for j, at, m in tiles_of(c):
                    mm = pe.matmul(bank[0:m, 6, j * P:(j + 1) * P], buf(q)[:, at:at + m], conv_w[:, w, :],
                                   start=True, stop=True)
                mm.then_inc(ph["table_made"], 1)
                reuse(pe, ph["loops_out"], c)
                pe.matmul(bank[:, 7, 0:n], conv_w[:, w, :], buf(q)[:, 0:n], start=True,
                          stop=True).then_inc(ph["loops_made"], 1)
            return stage

        def conv_rows_scalar(act, ph):
            def stage(c, q):
                n = width(c)
                act.wait_ge(ph["table_made"], c + 1)
                if not isinstance(c, int) or c >= 2:
                    act.wait_ge(ph["table_stored"][q], (c - q) * 8)
                for m, j0, j1 in [(P, 0, TILES)] if n == CHUNK else [(m, j, j + 1) for j, _, m in tiles_of(c)]:
                    op = act.copy(wide[0:m, q, j0 * P:j1 * P], bank[0:m, 6, j0 * P:j1 * P])
                op.then_inc(ph["table_out"], 1)
                act.wait_ge(ph["loops_made"], c + 1)
                act.copy(sums[:, 0, cols(c)], bank[:, 7, 0:n]).then_inc(ph["loops_out"], 1)
            return stage

        def conv_rows_store(sp, ph, table):
            def stage(c, q):
                gate(sp, (ph["table_out"], c + 1))
                move_rows(sp, c, table, wide[:, q, 0:CHUNK].rearrange("p (j d) -> p j d", d=P), False,
                          ph["table_stored"][q])
            return stage

        def stores_end(sp, sems):
            for u in range(2):
                sp.wait_ge(sems[u], 16 * moves(chunks - 1, u))

        def norm_vector(dve, ph, b):
            def stage(c, q):
                tiles = tiles_of(c)
                wait_chunk(dve, ph, c, q)
                dve.wait_ge(ph["rows_made"], c + 1)
                spans = [(P, 0, TILES)] if width(c) == CHUNK else [(m, j, j + 1) for j, _, m in tiles]
                for m, j0, j1 in spans:
                    r = node_in[0:m, q, j0:j1, :]
                    op = dve.tensor_tensor(r, r, bank[0:m, b, j0 * P:j1 * P].rearrange("p (j d) -> p j d", d=P), ALU.add)
                op.then_inc(ph["norm_step"], 1)
                dve.wait_ge(ph["norm_step"], c * 3 + 1)
                for j, _, m in tiles:
                    op = dve.bn_stats(stat[0:m, j, :], node_in[0:m, q, j, :])
                op.then_inc(ph["norm_step"], 1)
                gate(dve, (ph["norm_step"], c * 3 + 2))
                for j, _, m in tiles:
                    op = dve.bn_aggr(moments[0:m, j, :], stat[0:m, j, :])
                op.then_inc(ph["norm_step"], 1)
                dve.wait_ge(ph["rstd_ready"], c * 2 + 1)
                for m, j0, j1 in spans:
                    op = dve.reciprocal(rstd[0:m, j0:j1], rstd[0:m, j0:j1])
                op.then_inc(ph["rstd_ready"], 1)
                dve.wait_ge(ph["rstd_ready"], c * 2 + 2)
                for j, _, m in tiles:
                    op = dve.tensor_scalar(node_in[0:m, q, j, :], node_in[0:m, q, j, :], moments[0:m, j, 0:1],
                                           rstd[0:m, j:j + 1], ALU.subtract, ALU.mult)
                op.then_inc(ph["normed"], 1)
            return stage

        def norm_scalar(act, ph):
            def stage(c, q):
                act.wait_ge(ph["norm_step"], c * 3 + 3)
                for m, j0, j1 in [(P, 0, TILES)] if width(c) == CHUNK else [(m, j, j + 1) for j, _, m in tiles_of(c)]:
                    op = act.activation(rstd[0:m, j0:j1], moments[0:m, j0:j1, 1], ACT.Sqrt, bias=eps[0:m, 0:1])
                op.then_inc(ph["rstd_ready"], 1)
            return stage

        def normed_store(sp, ph, table):
            def stage(c, q):
                gate(sp, (ph["normed"], c + 1))
                move_rows(sp, c, table, node_in[:, q], False, ph["normed_stored"][q])
            return stage

        def load_again(sp, ph, table):
            def stage(c, q):
                if not isinstance(c, int) or c >= 2:
                    turned_too = [(ph["normed_turned"], c - 1)] if ph is update2 else []
                    gate(sp, (ph["normed_stored"][q], (c - q) * 8), *turned_too)
                move_rows(sp, c, table, node_in[:, q], True, ph["x_in"][q])
            return stage

        def out_rows_tensor(pe, ph, b, w, bias, lag_sem, wait_bank=None):
            def stage(c, q):
                pe.wait_ge(lag_sem, c + 1)
                if not isinstance(c, int) or c >= 1:
                    pe.wait_ge(ph["norm_step"], (c - 1) * 3 + 1)
                if wait_bank:
                    wait_bank(c)
                for j, at, m in tiles_of(c):
                    pe.matmul(bank[0:m, b, j * P:(j + 1) * P], left[:, q, at:at + m], w, start=True, stop=False)
                    mm = pe.matmul(bank[0:m, b, j * P:(j + 1) * P], ones[0:1, 0:m], bias, start=False, stop=True)
                mm.then_inc(ph["rows_made"], 1)
            return stage

        update2 = gru_phase("update2", ["rows_made", "norm_step", "rstd_ready", "normed", "normed_turned", "scaled",
                                        "kept", "table_made", "table_out", "loops_made", "loops_out", "inverted",
                                        "dinv_ready"])
        pair_sems(update2, "update2", ["x_in", "normed_stored", "table_stored"])

        def scaled_buf(q):
            return wide[:, q, CHUNK:2 * CHUNK]

        def update2_phase(engine, eng):
            ph = update2
            if engine == "sync":
                def end():
                    stores_end(eng, ph["normed_stored"])
                    stores_end(eng, ph["table_stored"])
                    state_stores_end(eng, ph)
                return [(load_state(eng, ph, "blended"), 0), (load_again(eng, ph, x), 0),
                        (normed_store(eng, ph, x1_dram), 1), (store_state(eng, ph, "kept", state_out), 1),
                        (conv_rows_store(eng, ph, conv_tables[0]), 2)], end
            if engine == "tensor":
                def rows_bank(c):
                    reuse(eng, ph["table_out"], c)

                def turn(c, q):
                    eng.wait_ge(ph["normed"], c + 1)
                    reuse(eng, ph["kept"], c)
                    reuse(eng, ph["loops_out"], c)
                    for j, at, m in tiles_of(c):
                        mm = eng.transpose(bank[:, 7, at:at + m], node_in[0:m, q, j, :], ident[0:m, 0:m])
                    mm.then_inc(ph["normed_turned"], 1)

                def conv_banks(c):
                    eng.wait_ge(ph["norm_step"], c * 3 + 1)
                    eng.wait_ge(ph["kept"], c + 1)
                return [(conv_rows_tensor(eng, ph, 0, scaled_buf, conv_banks), 2),
                        (out_rows_tensor(eng, ph, 6, out_wt[:, :], bias_rows[0:1, 0, :], ph["blended"], rows_bank), 1),
                        (gru_tensor(eng, ph, 1), 0), (turn, 1)], nothing
            if engine == "scalar":
                def dinv(c, q):
                    eng.wait_ge(ph["inverted"], c + 1)
                    eng.activation(sums[:, 1, cols(c)], sums[:, 1, cols(c)], ACT.Sqrt).then_inc(ph["dinv_ready"], 1)

                def keep(c, q):
                    n = width(c)
                    eng.wait_ge(ph["scaled"], c + 1)
                    buffer_stored(eng, ph["state_stored"], c, q)
                    eng.copy(state_out[:, q, 0:n], bank[:, 7, 0:n]).then_inc(ph["kept"], 1)
                return [(conv_rows_scalar(eng, ph), 2), (dinv, 0), (norm_scalar(eng, ph), 1),
                        (gru_scalar_gates(eng, ph, 1), 0), (gru_scalar_tanh(eng, ph, 1), 0), (keep, 1)], nothing
            if engine == "vector":
                def invert(c, q):
                    eng.reciprocal(sums[:, 1, cols(c)], sums[:, 1, cols(c)]).then_inc(ph["inverted"], 1)

                def scale(c, q):
                    n = width(c)
                    eng.wait_ge(ph["normed_turned"], c + 1)
                    eng.wait_ge(ph["dinv_ready"], c + 1)
                    reuse(eng, ph["loops_made"], c, 2)
                    eng.tensor_tensor(scaled_buf(q)[:, 0:n], bank[:, 7, 0:n], sums[:, 1, cols(c)],
                                      ALU.mult).then_inc(ph["scaled"], 1)

                def end():
                    eng.tensor_single_scalar(idx[:, :], idx[:, :], types_log2, ALU.logical_shift_right)
                blend = gru_vector_blend(eng, ph, lambda c, q: reuse(eng, ph["rows_made"], c, 2))
                return [(invert, 0), (norm_vector(eng, ph, 6), 1), (gru_vector_candidate(eng, ph, 1), 0), (blend, 0),
                        (scale, 1)], end
            return [], nothing

        def conv_phase_sems(tag):
            ph = phase_sems(tag, ["root_made", "conv_step", "kept", "scaled", "table_made", "table_out",
                                  "loops_made", "loops_out"])
            return pair_sems(ph, tag, ["table_stored", "state_loaded", "state_stored"])

        convs = [conv_phase_sems("conv1"), conv_phase_sems("conv2")]

        def conv_phase(engine, eng, k):
            ph, root, nxt = convs[k], 2 * k + 1, 2 * k + 2
            keeps = k == 0
            if engine == "sync":
                def end():
                    stores_end(eng, ph["table_stored"])
                    if keeps:
                        state_stores_end(eng, ph)
                keep = [(store_state(eng, ph, "kept", state_out), 1)] if keeps else []
                return [(load_state(eng, ph, "root_made"), 0)] + keep + [(conv_rows_store(eng, ph, conv_tables[(k + 1) % 2]), 1)], end
            if engine == "tensor":
                def root_term(c, q):
                    n = width(c)
                    reuse(eng, ph["conv_step"], c, 2, per=2)
                    eng.wait_ge(ph["state_loaded"][q], (c - q) * 8 + 16)
                    eng.matmul(bank[:, 2 + q, 0:n], conv_w[:, root, :], state_in[:, q, 0:n], start=True,
                               stop=True).then_inc(ph["root_made"], 1)
                return [(root_term, 0), (conv_rows_tensor(eng, ph, nxt, lambda q: left[:, q]), 1)], nothing
            if engine == "scalar":
                def keep(c, q):
                    n = width(c)
                    eng.wait_ge(ph["conv_step"], c * 2 + 2)
                    buffer_stored(eng, ph["state_stored"], c, q)
                    eng.activation(state_out[:, q, 0:n], tmp[:, q, 0:n], ACT.Relu).then_inc(ph["kept"], 1)
                return ([(keep, 0)] if keeps else []) + [(conv_rows_scalar(eng, ph), 1)], nothing
            if engine == "vector":
                def end(c, q):
                    n = width(c)
                    if keeps:
                        reuse(eng, ph["kept"], c, 2)
                    eng.tensor_tensor(tmp[:, q, 0:n], sums[:, 0, cols(c)], sums[:, 1, cols(c)],
                                      ALU.mult).then_inc(ph["conv_step"], 1)
                    eng.wait_ge(ph["conv_step"], c * 2 + 1)
                    eng.wait_ge(ph["root_made"], c + 1)
                    eng.tensor_tensor(tmp[:, q, 0:n], tmp[:, q, 0:n], bank[:, 2 + q, 0:n],
                                      ALU.add).then_inc(ph["conv_step"], 1)
                    eng.wait_ge(ph["conv_step"], c * 2 + 2)
                    reuse(eng, ph["loops_made"], c, 2)
                    eng.scalar_tensor_tensor(out=left[:, q, 0:n], in0=tmp[:, q, 0:n], scalar=0.0,
                                             in1=sums[:, 1, cols(c)], op0=ALU.max,
                                             op1=ALU.mult).then_inc(ph["scaled"], 1)
                return [(end, 0)], nothing
            return [], nothing

        final = phase_sems("final", ["conv_out", "rows_made", "norm_step", "rstd_ready", "normed"])
        pair_sems(final, "final", ["x_in", "normed_stored"])

        def final_phase(engine, eng):
            ph = final
            if engine == "sync":
                return [(load_again(eng, ph, x1_dram), 0), (normed_store(eng, ph, out), 1)], \
                    lambda: stores_end(eng, ph["normed_stored"])
            if engine == "tensor":
                return [(out_rows_tensor(eng, ph, 6, conv_w[:, 5, :], bias_rows[0:1, 1, :], ph["conv_out"]), 0)], nothing
            if engine == "scalar":
                return [(norm_scalar(eng, ph), 1)], nothing
            if engine == "vector":
                def last_conv(c, q):
                    n = width(c)
                    reuse(eng, ph["rows_made"], c, 2)
                    eng.tensor_tensor(left[:, q, 0:n], sums[:, 0, cols(c)], sums[:, 1, cols(c)],
                                      ALU.mult).then_inc(ph["conv_out"], 1)
                return [(last_conv, 0), (norm_vector(eng, ph, 6), 1)], nothing
            return [], nothing


        phases = [update1_phase, update2_phase, lambda e, eng: conv_phase(e, eng, 0),
                  lambda e, eng: conv_phase(e, eng, 1), final_phase]

        def following(engine, eng):
            for number, phase in enumerate(phases):
                stages, end = phase(engine, eng)
                if engine == "vector":
                    first_windows(eng)
                    eng.wait_ge(windows_set, number + 1)
                if engine in ("tensor", "vector"):
                    stages = [(edge_stage(engine, eng, number), 0)] + stages
                if engine == "pool":
                    edge_pool(eng, number, 1)
                if stages:
                    sweep(eng, stages)
                end()
                if number < len(phases) - 1:
                    barrier(eng, engine)

        def apart(engine, eng):
            rounds = eng.snap(eng.value_load(plan_cell[0:1, 0:1], min_val=1, max_val=nodes // WINDOW + 2))
            for number, phase in enumerate(phases):
                edge_rounds(engine, eng, number, rounds)
                barrier(eng, engine)
                stages, end = phase(engine, eng)
                if stages:
                    sweep(eng, stages)
                end()
                if number < len(phases) - 1:
                    barrier(eng, engine)

        def passes(engine, eng):
            stages, end = project_phase(engine, eng)
            if stages:
                sweep(eng, stages)
            end()
            if engine == "tensor":
                eng.sem_inc(group_done, TURN_GROUPS)
            if engine == "vector":
                eng.sem_inc(sums_added, 2)
            barrier(eng, engine)
            ordered = eng.snap(eng.value_load(plan_cell[0:1, 1:2], min_val=0, max_val=1))
            passed = phases_passed[engine]
            with eng.If_eq(eng.to_reg(ordered), 1):
                following(engine, eng)
            phases_passed[engine] = passed
            with eng.Else():
                apart(engine, eng)

        block = ctx.enter_context(nc.Block())

        @block.sync
        def _(sp):
            setup_sync(sp)
            gate(sp, (raw_turned, n_raw))
            passes("sync", sp)

        @block.gpsimd
        def _(pool):
            setup_pool(pool)
            passes("pool", pool)

        @block.scalar
        def _(act):
            for k, to in enumerate(raw_blocks):
                act.wait_ge(raw_turned, min(k // 4 * 4 + 4, n_raw))
                act.copy(to, raw_bank(k)).then_inc(raw_used, 1)
            act.wait_ge(bias_in, 16)
            passes("scalar", act)

        @block.vector
        def _(dve):
            setup_vector(dve)
            passes("vector", dve)

        @block.tensor
        def _(pe):
            setup_tensor(pe)
            passes("tensor", pe)


_INS = ['x', 'src', 'dst', 'edge_type_8', 'L0_gnn_node_proj_w', 'L0_gnn_node_proj_b', 'L0_gnn_edge_W',
        'L0_gnn_gru_wih', 'L0_gnn_gru_whh', 'L0_gnn_gru_bih', 'L0_gnn_gru_bhh', 'L0_gnn_out_w', 'L0_gnn_out_b',
        'L1_gnn_W1', 'L1_gnn_R1', 'L1_gnn_W2', 'L1_gnn_R2', 'L1_gnn_W3', 'L1_gnn_Wh', 'L1_gnn_bh']


def kernel(**inputs):
    import numpy as _np
    import concourse.bacc as _bacc
    from concourse import mybir as _mybir
    from concourse.bass_utils import run_bass_kernel_spmd as _run

    nc = _bacc.Bacc("TRN2", target_bir_lowering=False, num_devices=1)
    arrays, args = {}, []
    for name in _INS:
        a = _np.ascontiguousarray(inputs[name])
        arrays[f"in_{name}"] = a
        args.append(nc.dram_tensor(f"in_{name}", a.shape, _mybir.dt.from_np(a.dtype), kind="ExternalInput").ap())
    shape = tuple(inputs["x"].shape)
    args.append(nc.dram_tensor("out_0", shape, _mybir.dt.float32, kind="ExternalOutput").ap())
    gnn_kernel(nc, *args)
    r = _run(nc, [arrays], core_ids=[0])
    return r.results[0]["out_0"]
```
